# Optimizing a Trainium2 kernel written in Bass

```python
import numpy as np
import jax
import jax.numpy as jnp

def _softmax(x, axis=-1):
    return jax.nn.softmax(x, axis=axis)

def _gelu(x):
    return jax.nn.gelu(x, approximate=True)

def _silu(x):
    return jax.nn.silu(x)

def _sigmoid(x):
    return jax.nn.sigmoid(x)

def _layernorm(x, axis=-1, eps=1e-05):
    m = jnp.mean(x, axis=axis, keepdims=True)
    v = jnp.var(x, axis=axis, keepdims=True)
    return (x - m) / jnp.sqrt(v + eps)

def _scatter_add(tgt, idx, src, axis=0):
    return tgt.at[idx].add(src)

def _segment_sum(src, seg, n):
    return jax.ops.segment_sum(src, seg, n)
kernel_name = 'mk_dlrm_tower_d1_rec_r8_4650ed'

def setup_inputs(seed: int=0):
    np.random.seed(seed)
    _w = jnp.asarray

    def _rec_inputs():
        import jax
        import jax.numpy as jnp
        _tk = jax.random.key(seed)
        dense_ctx = jax.random.normal(jax.random.fold_in(_tk, 190), (2048, 16), jnp.float32)
        ids = jnp.stack([jax.random.randint(jax.random.fold_in(_tk, 200 + f), (2048,), 0, v, jnp.int32) for f, v in enumerate([125000, 1000, 1000, 125000, 125000, 1000, 1250, 1250, 1250, 12500, 1250, 1250, 12500, 1000, 125000, 12500, 12500, 1250, 125000, 1000, 1000, 12500, 1000, 125000, 1250, 1000, 125000, 1000, 12500, 125000, 12500, 125000, 12500, 12500, 125000, 12500, 125000, 12500, 1000])], axis=1)
        tbl_0 = 0.05 * jax.random.normal(jax.random.fold_in(_tk, 500 + 0), (125000, 16), jnp.float32)
        tbl_1 = 0.05 * jax.random.normal(jax.random.fold_in(_tk, 500 + 1), (1000, 16), jnp.float32)
        tbl_2 = 0.05 * jax.random.normal(jax.random.fold_in(_tk, 500 + 2), (1000, 16), jnp.float32)
        tbl_3 = 0.05 * jax.random.normal(jax.random.fold_in(_tk, 500 + 3), (125000, 16), jnp.float32)
        tbl_4 = 0.05 * jax.random.normal(jax.random.fold_in(_tk, 500 + 4), (125000, 16), jnp.float32)
        tbl_5 = 0.05 * jax.random.normal(jax.random.fold_in(_tk, 500 + 5), (1000, 16), jnp.float32)
        tbl_6 = 0.05 * jax.random.normal(jax.random.fold_in(_tk, 500 + 6), (1250, 16), jnp.float32)
        tbl_7 = 0.05 * jax.random.normal(jax.random.fold_in(_tk, 500 + 7), (1250, 16), jnp.float32)
        tbl_8 = 0.05 * jax.random.normal(jax.random.fold_in(_tk, 500 + 8), (1250, 16), jnp.float32)
        tbl_9 = 0.05 * jax.random.normal(jax.random.fold_in(_tk, 500 + 9), (12500, 16), jnp.float32)
        tbl_10 = 0.05 * jax.random.normal(jax.random.fold_in(_tk, 500 + 10), (1250, 16), jnp.float32)
        tbl_11 = 0.05 * jax.random.normal(jax.random.fold_in(_tk, 500 + 11), (1250, 16), jnp.float32)
        tbl_12 = 0.05 * jax.random.normal(jax.random.fold_in(_tk, 500 + 12), (12500, 16), jnp.float32)
        tbl_13 = 0.05 * jax.random.normal(jax.random.fold_in(_tk, 500 + 13), (1000, 16), jnp.float32)
        tbl_14 = 0.05 * jax.random.normal(jax.random.fold_in(_tk, 500 + 14), (125000, 16), jnp.float32)
        tbl_15 = 0.05 * jax.random.normal(jax.random.fold_in(_tk, 500 + 15), (12500, 16), jnp.float32)
        tbl_16 = 0.05 * jax.random.normal(jax.random.fold_in(_tk, 500 + 16), (12500, 16), jnp.float32)
        tbl_17 = 0.05 * jax.random.normal(jax.random.fold_in(_tk, 500 + 17), (1250, 16), jnp.float32)
        tbl_18 = 0.05 * jax.random.normal(jax.random.fold_in(_tk, 500 + 18), (125000, 16), jnp.float32)
        tbl_19 = 0.05 * jax.random.normal(jax.random.fold_in(_tk, 500 + 19), (1000, 16), jnp.float32)
        tbl_20 = 0.05 * jax.random.normal(jax.random.fold_in(_tk, 500 + 20), (1000, 16), jnp.float32)
        tbl_21 = 0.05 * jax.random.normal(jax.random.fold_in(_tk, 500 + 21), (12500, 16), jnp.float32)
        tbl_22 = 0.05 * jax.random.normal(jax.random.fold_in(_tk, 500 + 22), (1000, 16), jnp.float32)
        tbl_23 = 0.05 * jax.random.normal(jax.random.fold_in(_tk, 500 + 23), (125000, 16), jnp.float32)
        tbl_24 = 0.05 * jax.random.normal(jax.random.fold_in(_tk, 500 + 24), (1250, 16), jnp.float32)
        tbl_25 = 0.05 * jax.random.normal(jax.random.fold_in(_tk, 500 + 25), (1000, 16), jnp.float32)
        tbl_26 = 0.05 * jax.random.normal(jax.random.fold_in(_tk, 500 + 26), (125000, 16), jnp.float32)
        tbl_27 = 0.05 * jax.random.normal(jax.random.fold_in(_tk, 500 + 27), (1000, 16), jnp.float32)
        tbl_28 = 0.05 * jax.random.normal(jax.random.fold_in(_tk, 500 + 28), (12500, 16), jnp.float32)
        tbl_29 = 0.05 * jax.random.normal(jax.random.fold_in(_tk, 500 + 29), (125000, 16), jnp.float32)
        tbl_30 = 0.05 * jax.random.normal(jax.random.fold_in(_tk, 500 + 30), (12500, 16), jnp.float32)
        tbl_31 = 0.05 * jax.random.normal(jax.random.fold_in(_tk, 500 + 31), (125000, 16), jnp.float32)
        tbl_32 = 0.05 * jax.random.normal(jax.random.fold_in(_tk, 500 + 32), (12500, 16), jnp.float32)
        tbl_33 = 0.05 * jax.random.normal(jax.random.fold_in(_tk, 500 + 33), (12500, 16), jnp.float32)
        tbl_34 = 0.05 * jax.random.normal(jax.random.fold_in(_tk, 500 + 34), (125000, 16), jnp.float32)
        tbl_35 = 0.05 * jax.random.normal(jax.random.fold_in(_tk, 500 + 35), (12500, 16), jnp.float32)
        tbl_36 = 0.05 * jax.random.normal(jax.random.fold_in(_tk, 500 + 36), (125000, 16), jnp.float32)
        tbl_37 = 0.05 * jax.random.normal(jax.random.fold_in(_tk, 500 + 37), (12500, 16), jnp.float32)
        tbl_38 = 0.05 * jax.random.normal(jax.random.fold_in(_tk, 500 + 38), (1000, 16), jnp.float32)
        _rk = jax.random.fold_in(_tk, 7)
        W_top1 = 0.0606339 * jax.random.normal(jax.random.fold_in(_tk, 801), (272, 512), jnp.float32)
        W_top2 = 0.0441942 * jax.random.normal(jax.random.fold_in(_tk, 802), (512, 256), jnp.float32)
        W_top3 = 0.0625 * jax.random.normal(jax.random.fold_in(_tk, 803), (256, 1), jnp.float32)
        b_top1 = jnp.zeros((512,), jnp.float32)
        b_top2 = jnp.zeros((256,), jnp.float32)
        return (dense_ctx, ids, tbl_0, tbl_1, tbl_2, tbl_3, tbl_4, tbl_5, tbl_6, tbl_7, tbl_8, tbl_9, tbl_10, tbl_11, tbl_12, tbl_13, tbl_14, tbl_15, tbl_16, tbl_17, tbl_18, tbl_19, tbl_20, tbl_21, tbl_22, tbl_23, tbl_24, tbl_25, tbl_26, tbl_27, tbl_28, tbl_29, tbl_30, tbl_31, tbl_32, tbl_33, tbl_34, tbl_35, tbl_36, tbl_37, tbl_38, W_top1, b_top1, W_top2, b_top2, W_top3)
    dense_ctx, ids, tbl_0, tbl_1, tbl_2, tbl_3, tbl_4, tbl_5, tbl_6, tbl_7, tbl_8, tbl_9, tbl_10, tbl_11, tbl_12, tbl_13, tbl_14, tbl_15, tbl_16, tbl_17, tbl_18, tbl_19, tbl_20, tbl_21, tbl_22, tbl_23, tbl_24, tbl_25, tbl_26, tbl_27, tbl_28, tbl_29, tbl_30, tbl_31, tbl_32, tbl_33, tbl_34, tbl_35, tbl_36, tbl_37, tbl_38, W_top1, b_top1, W_top2, b_top2, W_top3 = _rec_inputs()

    def _L0_rec_setup():
        import jax, jax.numpy as jnp
        import numpy as np
        B, F0, D = (256, 39, 16)
        LAYER_SIZES = [128, 128, 128]
        key = jax.random.key(seed)
        ks = jax.random.split(key, 1 + 2 * len(LAYER_SIZES))
        inputs = jax.random.normal(ks[0], (B, F0, D), dtype=jnp.float32)
        out = {'inputs': inputs}
        field_nums = [F0]
        for i, size in enumerate(LAYER_SIZES):
            fk = field_nums[-1]
            fan_in = F0 * fk
            scale = np.sqrt(2.0 / (fan_in + size)).astype(np.float32)
            out[f'w{i}'] = jax.random.normal(ks[1 + 2 * i], (F0, fk, size), dtype=jnp.float32) * scale
            out[f'b{i}'] = jnp.zeros((size,), dtype=jnp.float32)
            field_nums.append(size // 2)
        return out
    _L0_rec_all = _L0_rec_setup()
    _L0_rec_in = {k: v for k, v in _L0_rec_all.items() if k in ('w0', 'w1', 'w2', 'b0', 'b1', 'b2')}
    del _L0_rec_all
    return {'dense_ctx': dense_ctx, 'ids': ids, 'tbl_0': tbl_0, 'tbl_1': tbl_1, 'tbl_2': tbl_2, 'tbl_3': tbl_3, 'tbl_4': tbl_4, 'tbl_5': tbl_5, 'tbl_6': tbl_6, 'tbl_7': tbl_7, 'tbl_8': tbl_8, 'tbl_9': tbl_9, 'tbl_10': tbl_10, 'tbl_11': tbl_11, 'tbl_12': tbl_12, 'tbl_13': tbl_13, 'tbl_14': tbl_14, 'tbl_15': tbl_15, 'tbl_16': tbl_16, 'tbl_17': tbl_17, 'tbl_18': tbl_18, 'tbl_19': tbl_19, 'tbl_20': tbl_20, 'tbl_21': tbl_21, 'tbl_22': tbl_22, 'tbl_23': tbl_23, 'tbl_24': tbl_24, 'tbl_25': tbl_25, 'tbl_26': tbl_26, 'tbl_27': tbl_27, 'tbl_28': tbl_28, 'tbl_29': tbl_29, 'tbl_30': tbl_30, 'tbl_31': tbl_31, 'tbl_32': tbl_32, 'tbl_33': tbl_33, 'tbl_34': tbl_34, 'tbl_35': tbl_35, 'tbl_36': tbl_36, 'tbl_37': tbl_37, 'tbl_38': tbl_38, 'W_top1': W_top1, 'b_top1': b_top1, 'W_top2': W_top2, 'b_top2': b_top2, 'W_top3': W_top3, 'L0_rec_w0': _L0_rec_in['w0'], 'L0_rec_w1': _L0_rec_in['w1'], 'L0_rec_w2': _L0_rec_in['w2'], 'L0_rec_b0': _L0_rec_in['b0'], 'L0_rec_b1': _L0_rec_in['b1'], 'L0_rec_b2': _L0_rec_in['b2']}

def reference(dense_ctx, ids, tbl_0, tbl_1, tbl_2, tbl_3, tbl_4, tbl_5, tbl_6, tbl_7, tbl_8, tbl_9, tbl_10, tbl_11, tbl_12, tbl_13, tbl_14, tbl_15, tbl_16, tbl_17, tbl_18, tbl_19, tbl_20, tbl_21, tbl_22, tbl_23, tbl_24, tbl_25, tbl_26, tbl_27, tbl_28, tbl_29, tbl_30, tbl_31, tbl_32, tbl_33, tbl_34, tbl_35, tbl_36, tbl_37, tbl_38, W_top1, b_top1, W_top2, b_top2, W_top3, L0_rec_w0, L0_rec_w1, L0_rec_w2, L0_rec_b0, L0_rec_b1, L0_rec_b2):
    import jax
    import jax.numpy as jnp

    def _L0_rec_ref(inputs, w0, w1, w2, b0, b1, b2):
        import jax, jax.numpy as jnp
        import numpy as np
        B, F0, D = (256, 39, 16)
        LAYER_SIZES = [128, 128, 128]
        x0 = inputs
        xk = inputs
        params = [(w0, b0), (w1, b1), (w2, b2)]
        n_layers = len(params)
        direct = []
        for idx, (W, b) in enumerate(params):
            z = jnp.einsum('bhd,bkd,hks->bsd', x0, xk, W) + b[None, :, None]
            z = jax.nn.relu(z)
            if idx != n_layers - 1:
                half = z.shape[1] // 2
                xk = z[:, :half, :]
                direct.append(z[:, half:, :])
            else:
                direct.append(z)
        logit = jnp.sum(jnp.concatenate(direct, axis=1), axis=-1)
        return logit
    e = jnp.stack([tbl_0[ids[:, 0]], tbl_1[ids[:, 1]], tbl_2[ids[:, 2]], tbl_3[ids[:, 3]], tbl_4[ids[:, 4]], tbl_5[ids[:, 5]], tbl_6[ids[:, 6]], tbl_7[ids[:, 7]], tbl_8[ids[:, 8]], tbl_9[ids[:, 9]], tbl_10[ids[:, 10]], tbl_11[ids[:, 11]], tbl_12[ids[:, 12]], tbl_13[ids[:, 13]], tbl_14[ids[:, 14]], tbl_15[ids[:, 15]], tbl_16[ids[:, 16]], tbl_17[ids[:, 17]], tbl_18[ids[:, 18]], tbl_19[ids[:, 19]], tbl_20[ids[:, 20]], tbl_21[ids[:, 21]], tbl_22[ids[:, 22]], tbl_23[ids[:, 23]], tbl_24[ids[:, 24]], tbl_25[ids[:, 25]], tbl_26[ids[:, 26]], tbl_27[ids[:, 27]], tbl_28[ids[:, 28]], tbl_29[ids[:, 29]], tbl_30[ids[:, 30]], tbl_31[ids[:, 31]], tbl_32[ids[:, 32]], tbl_33[ids[:, 33]], tbl_34[ids[:, 34]], tbl_35[ids[:, 35]], tbl_36[ids[:, 36]], tbl_37[ids[:, 37]], tbl_38[ids[:, 38]]], axis=1)
    z = _L0_rec_ref(e, L0_rec_w0, L0_rec_w1, L0_rec_w2, L0_rec_b0, L0_rec_b1, L0_rec_b2)
    z = z.reshape(z.shape[0], -1)
    h = jnp.concatenate([z, dense_ctx], axis=1)
    h = jnp.maximum(h @ W_top1 + b_top1, 0.0)
    h = jnp.maximum(h @ W_top2 + b_top2, 0.0)
    y = h @ W_top3
    return y

_drawn_inputs = setup_inputs


def setup_inputs(seed=0):
    import zlib

    import numpy as np

    out = dict(_drawn_inputs(seed))
    spreads = {'b_top1': (0.0, 2.0),
     'b_top2': (0.0, 2.0),
     'L0_rec_b0': (0.0, 0.341),
     'L0_rec_b1': (0.0, 0.538),
     'L0_rec_b2': (0.0, 0.8)}
    factors = {'tbl_0': 8.0,
     'tbl_1': 8.0,
     'tbl_2': 8.0,
     'tbl_3': 8.0,
     'tbl_4': 8.0,
     'tbl_5': 8.0,
     'tbl_6': 8.0,
     'tbl_7': 8.0,
     'tbl_8': 8.0,
     'tbl_9': 8.0,
     'tbl_10': 8.0,
     'tbl_11': 8.0,
     'tbl_12': 8.0,
     'tbl_13': 8.0,
     'tbl_14': 8.0,
     'tbl_15': 8.0,
     'tbl_16': 8.0,
     'tbl_17': 8.0,
     'tbl_18': 8.0,
     'tbl_19': 8.0,
     'tbl_20': 8.0,
     'tbl_21': 8.0,
     'tbl_22': 8.0,
     'tbl_23': 8.0,
     'tbl_24': 8.0,
     'tbl_25': 8.0,
     'tbl_26': 8.0,
     'tbl_27': 8.0,
     'tbl_28': 8.0,
     'tbl_29': 8.0,
     'tbl_30': 8.0,
     'tbl_31': 8.0,
     'tbl_32': 8.0,
     'tbl_33': 8.0,
     'tbl_34': 8.0,
     'tbl_35': 8.0,
     'tbl_36': 8.0,
     'tbl_37': 8.0,
     'tbl_38': 8.0,
     'L0_rec_w0': 8.0,
     'L0_rec_w1': 6.243,
     'L0_rec_w2': 4.797,
     'dense_ctx': 8.0}
    for name, (base, spread) in spreads.items():
        noise = np.random.default_rng([zlib.crc32(name.encode()), seed]).standard_normal(out[name].shape)
        drawn = base * np.exp(spread * noise) if base else spread * noise
        out[name] = jnp.asarray(drawn.astype(out[name].dtype))
    for name, factor in factors.items():
        out[name] = (out[name] * factor).astype(out[name].dtype)
    return out
```

```python
from contextlib import ExitStack

import concourse.bass as bass
from concourse import mybir

F32 = mybir.dt.float32
F32R = mybir.dt.float32r
I32 = mybir.dt.int32
ALU = mybir.AluOpType
ACT = mybir.ActivationFunctionType

P = 128
FIELDS = 39
D = 16
BATCH = 2048
HALF = 64
BLOCKS = BATCH // P
CHUNK = 512
DPC = CHUNK // P
STEPS = D // DPC
BCOLS = D * P
PITCH = BATCH * D + 1024
TILES = 20
SHIFTS = 3
TILES0 = 7
ROWS0 = SHIFTS * FIELDS
LAST0 = 2 * FIELDS

PAIRS = [("F", 0), ("F", 1), ("D", 0), ("P", 0), ("D", 1), ("P", 1), ("D", 2), ("P", 2), ("D", 3), ("P", 3)]
PAIRS0 = [("P", 0), ("P", 1), ("F", 0), ("F", 1)]
ORDER = [0, 1, 2, 3, 4, 5, 6, 7, 8, 9]
ORDER0 = [0, 1, 2, 3]
PER_STEP = {"F": 6, "D": 8, "P": 10}
AHEAD = {"F": 2, "D": 0, "P": 2}
BEFORE = {
    "F": {1: 0, 0: 2, 2: 4},
    "D": {1: 0, 0: 4, 2: 4},
    "P": {1: 0, 0: 4, 2: 6},
}
RF, RPZ, RPH, RPL, RDH, RDL = 3, 2, 4, 2, 2, 2
DOUBLE = 5
EARLY = 18


def build(nc, ins, y_out):
    x0_dram = nc.dram_tensor("x0_scratch", [2 * FIELDS, PITCH], F32).ap()
    w0c_dram = nc.dram_tensor("w0_columns_twice", [FIELDS, 2 * FIELDS, P], F32).ap()
    w0r_dram = nc.dram_tensor("w0_rows_twice", [2 * FIELDS, FIELDS, P], F32).ap()

    with ExitStack() as ctx:
        def sb(name, shape, dt=F32):
            return ctx.enter_context(nc.sbuf_tensor(name, shape, dt))

        def ps(name, shape):
            return ctx.enter_context(nc.psum_tensor(name, shape, F32))

        def sem(name):
            return ctx.enter_context(nc.semaphore(name))

        bcA = sb("bcA", [P, 2, 2 * DOUBLE, CHUNK])
        bcB = sb("bcB", [P, TILES - 2 * DOUBLE, CHUNK])
        rot = sb("rot", [ROWS0, TILES0, CHUNK])
        rep = sb("rep", [ROWS0, CHUNK])
        zF = sb("zF", [P, RF, 2, CHUNK])
        zP = sb("zP", [P, RPZ, 2, CHUNK])
        hiP = sb("hiP", [P, RPH, 2, CHUNK], F32R)
        loP = sb("loP", [P, RPL, 2, CHUNK], F32R)
        hiD = sb("hiD", [P, RDH, 2, CHUNK], F32R)
        loD = sb("loD", [P, RDL, 2, CHUNK], F32R)
        n_f, n_r = 3 + 4 + 4, 4 + 16 + 16
        wF = sb("wF", [P, n_f, P])
        wH = sb("wH", [P, n_r, P], F32R)
        wL = sb("wL", [P, n_r, P], F32R)
        columns = sb("columns", [P, 11])
        bias, bt1, bt2, wt3 = columns[:, 0:3], columns[:, 3:7], columns[:, 7:9], columns[:, 9:11]
        ids_sb = sb("ids_sb", [P, FIELDS], I32)
        emb = sb("emb", [P, FIELDS, D])
        dense = sb("dense", [P, D])
        ident = sb("ident", [P, P])
        x0T = sb("x0T", [FIELDS, 2, CHUNK])
        denseT = sb("denseT", [D, P])
        sum01 = sb("sum01", [P, CHUNK])
        sum2 = sb("sum2", [P, CHUNK])
        dir01 = sb("dir01", [P, CHUNK])
        dir2 = sb("dir2", [P, CHUNK])
        zsum = sb("zsum", [P, 2, P])
        wt1 = sb("wt1", [P, 2, 512])
        wt1d = sb("wt1d", [D, 512])
        wt2 = sb("wt2", [P, 4, 256])
        h1 = sb("h1", [P, 4, P])
        h2 = sb("h2", [P, 2, P])
        y_sb = sb("y_sb", [1, P])

        acc = ps("acc", [P, 2, CHUNK])
        xk1 = ps("xk1", [P, CHUNK])
        xk2 = ps("xk2", [P, CHUNK])
        repP = ps("repP", [P, CHUNK])
        zD = ps("zD", [P, 2, CHUNK])
        misc = ps("misc", [P, CHUNK])

        stage = bcA[:, :, :, :].rearrange("p a t n -> p (a t n)")
        raw1 = stage[:, 0:TILES * P].rearrange("p (t s) -> p t s", s=P)
        raw2 = stage[:, TILES * P:2 * TILES * P].rearrange("p (t s) -> p t s", s=P)
        o = 2 * TILES * P
        symA = stage[:ROWS0, o:o + TILES0 * P].rearrange("p (t s) -> p t s", s=P)
        symB = stage[:ROWS0, o + TILES0 * P:o + 2 * TILES0 * P].rearrange("p (t s) -> p t s", s=P)

        s_w0c = sem("s_w0_columns_twice")
        s_w0r = sem("s_w0_rows_twice")
        s_sym = sem("s_sym_in")
        s_raw = sem("s_raw_in")
        s_small = sem("s_small_in")
        s_edge = sem("s_edge_zeroed")
        s_added = sem("s_sym_added")
        s_wh = sem("s_weights_hi")
        s_wl = sem("s_weights_split")
        s_id0 = sem("s_ident_zeroed")
        s_id = sem("s_ident_ready")
        s_ids = sem("s_ids_in")
        s_gather = sem("s_gathered")
        s_tr = sem("s_transposed")
        s_trout = sem("s_transposes_read")
        s_x0w = [sem(f"s_x0_written{g}") for g in range(STEPS)]
        s_dense = sem("s_dense_in")
        s_rot = sem("s_rot_in")
        s_rep = sem("s_rep_in_psum")
        s_bcA = [sem(f"s_bcA_in{p}") for p in range(2)]
        s_bcB = [sem(f"s_bcB_in{p}") for p in range(2)]
        s_mulF = sem("s_mulF")
        s_mulP = sem("s_mulP")
        s_mulD = sem("s_mulD")
        s_hiP = sem("s_hiP")
        s_hiD = sem("s_hiD")
        s_loP = sem("s_loP")
        s_loD = sem("s_loD")
        s_usedF = sem("s_usedF")
        s_usedP = sem("s_usedP")
        s_usedD = sem("s_usedD")
        s_out = sem("s_acc_read")
        s_xk1 = sem("s_xk1_ready")
        s_xk2 = sem("s_xk2_ready")
        s_add01 = sem("s_dir01_added")
        s_add2 = sem("s_dir2_added")
        s_half01 = sem("s_sum01_halved")
        s_half2 = sem("s_sum2_halved")
        s_z01 = sem("s_zsum01_ready")
        s_z2 = sem("s_zsum2_ready")
        s_top = sem("s_top_psum")
        s_topr = sem("s_top_read")
        s_y = sem("s_y_out")

        class Step:

            def __init__(self, b, k, tail=False):
                self.b, self.k, self.tail = b, k, tail

            def n(self, kind, layer, i):
                cut = AHEAD[kind] if self.tail and layer == 2 else 0
                return AHEAD[kind] + PER_STEP[kind] * self.k + BEFORE[kind][layer] + i - cut

            def count(self, kind, local):
                return PER_STEP[kind] * STEPS * self.b + local

            def stage(self, layer):
                return 1 + 3 * self.k + {1: 0, 0: 1, 2: 2}[layer] - (1 if self.tail and layer == 2 else 0)

            def steps(self):
                return self.b * STEPS + self.k

        class Ahead(Step):

            def __init__(self):
                super().__init__(0, 0)

            def n(self, kind, layer, i):
                return i

            def stage(self, layer):
                return 0

            def steps(self):
                return -1

        def wait_count(eng, s, value):
            if isinstance(value, int) and value <= 0:
                return
            eng.wait_ge(s, value)

        def in_registers(eng, *values):
            return [v if isinstance(v, int) else eng.to_reg(v) for v in values]

        def pairs_of(layer):
            return PAIRS0 if layer == 0 else PAIRS

        def tiles_of(layer, pos):
            return 1 if layer == 0 and pos == 3 else 2

        def rows_of(layer, pos):
            return P if layer else (LAST0 if pos == 3 else ROWS0)

        def bc_pair(st, pos):
            if pos < DOUBLE:
                return bcA[:, st.k % 2, 2 * pos:2 * pos + 2, :]
            q = pos - DOUBLE
            return bcB[:, 2 * q:2 * q + 2, :]

        def weight(layer, pos, j):
            kind, i = pairs_of(layer)[pos]
            if kind == "F":
                return kind, {0: 0, 1: 3, 2: 7}[layer] + 2 * i + j
            if layer == 0:
                return kind, 2 * pos + j
            return kind, 4 + 16 * (layer - 1) + 2 * (pos - 2) + j

        def run(engine, body):
            body(0)
            with engine.Fori(1, BLOCKS - 1) as b:
                body(b)
            body(BLOCKS - 1)

        def first(b):
            return isinstance(b, int) and b == 0

        def last(b):
            return isinstance(b, int) and b == BLOCKS - 1

        def is_tail(b, k):
            return last(b) and k == STEPS - 1

        block = ctx.enter_context(nc.Block())

        @block.sync
        def _(sp):
            def load_ids(b):
                sp.dma_start(ids_sb[:, :], ins["ids"][bass.ds(b * P, P), :]).then_inc(s_ids, 16)

            def load_dense(b):
                sp.dma_start(dense[:, :], ins["dense_ctx"][bass.ds(b * P, P), :]).then_inc(s_dense, 16)

            def x0_rows(row, col, dims):
                return bass.AP(tensor=x0_dram.tensor, offset=col + row * PITCH, ap=dims)

            def load_rot(b, k):
                col = b * BCOLS + k * CHUNK
                for j in range(SHIFTS):
                    sp.dma_start(rot[j * FIELDS:(j + 1) * FIELDS, :, :],
                                 x0_rows(j, col, [[PITCH, FIELDS], [SHIFTS * PITCH, TILES0], [1, CHUNK]])
                                 ).then_inc(s_rot, 16)
                for j in range(SHIFTS):
                    sp.dma_start(rep[j * FIELDS:(j + 1) * FIELDS, :],
                                 x0_rows(0, col, [[PITCH, FIELDS], [1, CHUNK]])).then_inc(s_rot, 16)

            def load_bcA(b, k):
                col = b * BCOLS + k * CHUNK
                for h in range(2):
                    sp.dma_start(bcA[h * HALF:(h + 1) * HALF, k % 2, :, :],
                                 x0_rows(h, col, [[0, HALF], [2 * PITCH, 2 * DOUBLE], [1, CHUNK]])
                                 ).then_inc(s_bcA[k % 2], 16)

            def load_bcB(b, k, part):
                lo, hi = [(DOUBLE, 7), (7, 10)][part]
                col = b * BCOLS + k * CHUNK
                for h in range(2):
                    sp.dma_start(bcB[h * HALF:(h + 1) * HALF, 2 * (lo - DOUBLE):2 * (hi - DOUBLE), :],
                                 x0_rows(4 * lo + h, col, [[0, HALF], [2 * PITCH, 2 * (hi - lo)], [1, CHUNK]])
                                 ).then_inc(s_bcB[part], 16)

            def write_x0(b, g):
                col = b * BCOLS + g * CHUNK
                for twice in range(2):
                    sp.dma_start(x0_dram[twice * FIELDS:(twice + 1) * FIELDS, bass.ds(col, CHUNK)],
                                 x0T[:, g % 2, :]).then_inc(s_x0w[g], 16)

            load_ids(0)
            w0 = ins["L0_rec_w0"]
            for twice in range(2):
                sp.dma_start(w0c_dram[:, twice * FIELDS:(twice + 1) * FIELDS, :], w0).then_inc(s_w0c, 16)
                sp.dma_start(w0r_dram[twice * FIELDS:(twice + 1) * FIELDS, :, :], w0).then_inc(s_w0r, 16)
            for layer, raw in ((1, raw1), (2, raw2)):
                w = ins[f"L0_rec_w{layer}"].rearrange("h k s -> (h k) s")
                sp.dma_start(raw[:, 0:TILES - 1, :],
                             w[0:(TILES - 1) * P, :].rearrange("(t p) s -> p t s", p=P)).then_inc(s_raw, 16)
                sp.dma_start(raw[0:HALF, TILES - 1, :], w[(TILES - 1) * P:FIELDS * HALF, :]).then_inc(s_raw, 16)
                sp.dma_start(wF[:, 4 * layer - 1:4 * layer + 3, :],
                             w[0:4 * P, :].rearrange("(t p) s -> p t s", p=P)).then_inc(s_raw, 16)
            sp.wait_ge(s_w0c, 32)
            sp.wait_ge(s_w0r, 32)
            for j in range(SHIFTS):
                sp.dma_start(symA[j * FIELDS:(j + 1) * FIELDS, :, :],
                             bass.AP(tensor=w0c_dram.tensor, offset=j * P,
                                     ap=[[(2 * FIELDS + 1) * P, FIELDS], [SHIFTS * P, TILES0], [1, P]])
                             ).then_inc(s_sym, 16)
                sp.dma_start(symB[j * FIELDS:(j + 1) * FIELDS, :, :],
                             bass.AP(tensor=w0r_dram.tensor, offset=j * FIELDS * P,
                                     ap=[[(FIELDS + 1) * P, FIELDS], [SHIFTS * FIELDS * P, TILES0], [1, P]])
                             ).then_inc(s_sym, 16)
            sp.dma_start(columns[:, :], ins["columns"]).then_inc(s_small, 16)
            sp.dma_start(wt1[:, :, :], ins["W_top1"][0:2 * P, :].rearrange("(t p) n -> p t n", p=P)).then_inc(s_small, 16)
            sp.dma_start(wt1d[:, :], ins["W_top1"][2 * P:2 * P + D, :]).then_inc(s_small, 16)
            sp.dma_start(wt2[:, :, :], ins["W_top2"].rearrange("(t p) n -> p t n", p=P)).then_inc(s_small, 16)

            for g in range(STEPS):
                sp.wait_ge(s_trout, g + 1)
                write_x0(0, g)
                if g == 0:
                    sp.wait_ge(s_x0w[0], 32)
                    load_rot(0, 0)
            sp.wait_ge(s_gather, 16 * FIELDS)
            load_ids(1)
            sp.wait_ge(s_wl, 3)
            load_bcA(0, 0)
            load_bcB(0, 0, 0)
            load_bcB(0, 0, 1)
            sp.wait_ge(s_mulF, 2)
            sp.wait_ge(s_x0w[1], 32)
            load_rot(0, 1)

            def body(b):
                for k in range(STEPS):
                    st = Step(b, k, is_tail(b, k))
                    nb, nk = (b, k + 1) if k < STEPS - 1 else (b + 1, 0)
                    rb, rk = (b, k + 2) if k < STEPS - 2 else (b + 1, k - 2)
                    if not is_tail(b, k):
                        used, written = in_registers(sp, st.count("D", st.n("D", 1, 0) - 2), 32 * nb + 32)
                        wait_count(sp, s_mulD, used)
                        sp.wait_ge(s_x0w[nk], written)
                        load_bcA(nb, nk)
                    if k == 0:
                        wait_count(sp, s_tr, 5 * b + 4)
                        load_dense(b)
                    if k == 1 and not first(b):
                        sp.wait_ge(s_topr, 3 * b)
                        sp.dma_start(y_out[bass.ds(b * P - P, P), :].rearrange("n a -> a n"), y_sb[:, :]).then_inc(s_y, 16)
                    if k == 2 and not last(b):
                        sp.wait_ge(s_gather, (16 * FIELDS) * b + 2 * 16 * FIELDS)
                        load_ids(b + 2)
                        for g in range(STEPS):
                            sp.wait_ge(s_trout, 5 * b + 4 + g + 1)
                            write_x0(b + 1, g)
                    if not (last(b) and k >= STEPS - 2):
                        used, written = in_registers(sp, st.count("F", st.n("F", 0, 1) + 1), 32 * rb + 32)
                        sp.wait_ge(s_mulF, used)
                        sp.wait_ge(s_x0w[rk], written)
                        load_rot(rb, rk)
                    if not is_tail(b, k):
                        sp.wait_ge(s_mulD, st.count("D", st.n("D", 2, 2) + 1))
                        load_bcB(nb, nk, 0)
                        sp.wait_ge(s_mulP, st.count("P", st.n("P", 2, 3) + 1))
                        load_bcB(nb, nk, 1)

            run(sp, body)
            sp.wait_ge(s_topr, 3 * BLOCKS)
            sp.dma_start(y_out[BATCH - P:BATCH, :].rearrange("n a -> a n"), y_sb[:, :]).then_inc(s_y, 16)
            sp.wait_ge(s_y, 16 * BLOCKS)

        @block.gpsimd
        def _(pool):
            nc.gpsimd.memset(ident[:, :], 0.0).then_inc(s_id0, 1)
            pool.wait_ge(s_id0, 1)
            nc.gpsimd.affine_select(out=ident[:, :], in_=ident[:, :], compare_op=ALU.not_equal, fill=1.0, base=0,
                                    pattern=[[-1, P]], channel_multiplier=1).then_inc(s_id, 1)

            def gather(field):
                pool.indirect_dma_start(emb[:, field, :], None, ins[f"tbl_{field}"][:, :],
                                        bass.IndirectOffsetOnAxis(ap=ids_sb[:, field:field + 1], axis=0)
                                        ).then_inc(s_gather, 16)

            def low(st, layer, i):
                n = st.n("P", layer, i)
                rows = P if layer else ROWS0
                pool.wait_ge(s_hiP, st.count("P", n + 1))
                wait_count(pool, s_usedP, st.count("P", n + 1 - RPL))
                nc.gpsimd.tensor_tensor(loP[:rows, n % RPL, :, :], zP[:rows, n % RPZ, :, :],
                                        hiP[:rows, n % RPH, :, :].bitcast(F32), ALU.subtract).then_inc(s_loP, 1)

            def finish2(b):
                pool.wait_ge(s_out, 12 * b + 13 - (1 if last(b) else 0))
                pool.wait_ge(s_add2, 3 * b + 2)
                nc.gpsimd.tensor_tensor(sum2[:, :], sum2[:, :], dir2[:, :], ALU.add).then_inc(s_add2, 1)
                pool.wait_ge(s_add2, 3 * b + 3)
                nc.gpsimd.tensor_tensor(sum2[:, 0:2 * P], sum2[:, 0:2 * P], sum2[:, 2 * P:4 * P],
                                        ALU.add).then_inc(s_half2, 1)
                pool.wait_ge(s_half2, b + 1)
                nc.gpsimd.tensor_tensor(zsum[:, 1, :], sum2[:, 0:P], sum2[:, P:2 * P], ALU.add).then_inc(s_z2, 1)

            pool.wait_ge(s_ids, 16)
            for f in range(FIELDS):
                gather(f)
            for i in range(2):
                low(Ahead(), 0, i)

            def body(b):
                late = [] if last(b) else list(range(0 if first(b) else EARLY, FIELDS))
                early = [] if last(b) else list(range(EARLY))

                def gathers(k, s):
                    todo, q, slots = (late, s + 10 * k, 20) if k < 2 else (early, s + 10 * (k - 2) - 2, 18)
                    fields = [] if q < 0 else todo[q * len(todo) // slots:(q + 1) * len(todo) // slots]
                    if first(b) and k == 0 and s == 0:
                        pool.wait_ge(s_ids, 32)
                        pool.wait_ge(s_tr, 4)
                    for f in fields:
                        gather(f)

                for k in range(STEPS):
                    st = Step(b, k, is_tail(b, k))
                    for i in range(4):
                        if k == 2 and i == 2 and not last(b):
                            pool.wait_ge(s_ids, 16 * b + 48)
                            pool.wait_ge(s_tr, 5 * b + 8)
                        low(st, 1, i)
                        gathers(k, i)
                        if i == 0 and k == 0 and not first(b):
                            finish2(b - 1)
                        if i == 0 and k >= 2:
                            pool.wait_ge(s_out, 12 * b + st.stage(1))
                            pool.wait_ge(s_add2, 3 * b + k - 2) if k == 3 else wait_count(pool, s_add2, 3 * b)
                            nc.gpsimd.tensor_tensor(sum2[:, :], sum2[:, :], dir2[:, :], ALU.add).then_inc(s_add2, 1)
                    if not is_tail(b, k):
                        for i in range(2):
                            low(st, 0, i)
                            gathers(k, 4 + i)
                    if k > 0:
                        pool.wait_ge(s_out, 12 * b + st.stage(1) + 1)
                        wait_count(pool, s_add01, 3 * b + k - 1)
                        nc.gpsimd.tensor_tensor(sum01[:, :], sum01[:, :], dir01[:, :], ALU.add).then_inc(s_add01, 1)
                    if k == STEPS - 1:
                        pool.wait_ge(s_add01, 3 * b + 3)
                        nc.gpsimd.tensor_tensor(sum01[:, 0:2 * P], sum01[:, 0:2 * P], sum01[:, 2 * P:4 * P],
                                                ALU.add).then_inc(s_half01, 1)
                        pool.wait_ge(s_half01, b + 1)
                        nc.gpsimd.tensor_tensor(zsum[:, 0, :], sum01[:, 0:P], sum01[:, P:2 * P],
                                                ALU.add).then_inc(s_z01, 1)
                    for i in range(4):
                        low(st, 2, i)
                        gathers(k, 6 + i)

            run(pool, body)
            finish2(BLOCKS - 1)

        @block.scalar
        def _(act):
            act.wait_ge(s_added, 1)
            nc.scalar.activation(wH[:ROWS0, 0:4, :], symA[:, 0:4, :], ACT.Copy).then_inc(s_wh, 1)
            act.wait_ge(s_raw, 96)
            act.wait_ge(s_edge, 1)
            for layer, raw in ((1, raw1), (2, raw2)):
                nc.scalar.activation(wH[:, 16 * layer - 12:16 * layer + 4, :], raw[:, 4:TILES, :],
                                     ACT.Copy).then_inc(s_wh, 1)

            def high(st, layer, kind, i):
                n = st.n(kind, layer, i)
                rows = P if layer else ROWS0
                if kind == "P":
                    act.wait_ge(s_mulP, st.count("P", n + 1))
                    wait_count(act, s_usedP, st.count("P", n + 1 - RPH))
                    nc.scalar.activation(hiP[:rows, n % RPH, :, :], zP[:rows, n % RPZ, :, :],
                                         ACT.Copy).then_inc(s_hiP, 1)
                else:
                    act.wait_ge(s_mulD, st.count("D", n + 1))
                    wait_count(act, s_usedD, st.count("D", n + 1 - RDH))
                    nc.scalar.activation(hiD[:, n % RDH, :, :], zD[:, :, :], ACT.Copy).then_inc(s_hiD, 1)

            def maps(st, layer, b, k):
                n = st.stage(layer)
                kind, i = pairs_of(layer)[(ORDER if layer else ORDER0)[-1]]
                act.wait_ge({"F": s_usedF, "D": s_usedD, "P": s_usedP}[kind], st.count(kind, st.n(kind, layer, i) + 1))
                src = acc[:, n % 2, :]
                if layer < 2:
                    xk, ready = ((xk1, s_xk1), (xk2, s_xk2))[layer]
                    for h in range(2):
                        nc.scalar.activation(xk[h * HALF:(h + 1) * HALF, :], src[0:HALF, :], ACT.Relu,
                                             bias=bias[0:HALF, layer:layer + 1]).then_inc(ready, 1)
                    wait_count(act, s_z01, b) if k == 0 else wait_count(act, s_add01, 3 * b + k - 1)
                    dst = sum01 if k == 0 else dir01
                    nc.scalar.activation(dst[layer * HALF:(layer + 1) * HALF, :], src[HALF:P, :], ACT.Relu,
                                         bias=bias[HALF:P, layer:layer + 1]).then_inc(s_out, 1)
                else:
                    wait_count(act, s_z2, b) if k == 0 else wait_count(act, s_add2, 3 * b + k - 1)
                    dst = sum2 if k == 0 else dir2
                    nc.scalar.activation(dst[:, :], src, ACT.Relu, bias=bias[:, 2:3]).then_inc(s_out, 1)

            def rep_to_psum(c):
                act.wait_ge(s_rot, 96 * c + 96)
                nc.scalar.activation(repP[:ROWS0, :], rep[:, :], ACT.Copy).then_inc(s_rep, 1)

            def transposed(b, g, n):
                act.wait_ge(s_tr, n)
                wait_count(act, s_x0w[(g - 2) % STEPS], 32 * b + (32 if g >= 2 else 0))
                nc.scalar.activation(x0T[:, g % 2, :], misc[:FIELDS, :], ACT.Copy).then_inc(s_trout, 1)

            for g in range(STEPS):
                transposed(0, g, g + 1)
            rep_to_psum(0)
            act.wait_ge(s_small, 64)
            for i in range(2):
                high(Ahead(), 0, "P", i)
            maps(Ahead(), 0, 0, 0)

            def relu_top(dst, n, b_col):
                for m in range(n):
                    a = nc.scalar.activation(dst[:, m, :], misc[:, m * P:(m + 1) * P], ACT.Relu,
                                             bias=b_col[:, m:m + 1])
                return a

            def body(b):
                for k in range(STEPS):
                    st = Step(b, k, is_tail(b, k))
                    for pos, (kind, i) in enumerate(PAIRS):
                        if kind == "F":
                            continue
                        high(st, 1, kind, i)
                        if (kind, i) == ("P", 0) and not (first(b) and k == 0):
                            before = Step(b, k - 1) if k else Step(b - 1, STEPS - 1)
                            maps(before, 2, before.b, before.k)
                        if (kind, i) == ("P", 0) and k == 1 and not first(b):
                            act.wait_ge(s_top, 3 * b)
                            wait_count(act, s_y, 16 * b - 16)
                            nc.scalar.activation(y_sb[:, :], misc[0:1, 0:P], ACT.Copy).then_inc(s_topr, 1)
                        if (kind, i) == ("P", 1) and not is_tail(b, k):
                            rep_to_psum(st.steps() + 1)
                        if kind == "P" and k == 2 and not last(b):
                            transposed(b + 1, i, 5 * b + 4 + i + 1)
                    if not is_tail(b, k):
                        for i in range(2):
                            high(st, 0, "P", i)
                    maps(st, 1, b, k)
                    if k == 0 and not first(b):
                        act.wait_ge(s_top, 3 * b - 2)
                        relu_top(h1, 4, bt1).then_inc(s_topr, 1)
                    if k == 2:
                        act.wait_ge(s_tr, 5 * b + (5 if last(b) else 9))
                        wait_count(act, s_top, 3 * b - 2)
                        nc.scalar.activation(denseT[:, :], misc[:D, 0:P], ACT.Copy).then_inc(s_trout, 1)
                    for pos, (kind, i) in enumerate(PAIRS):
                        if kind == "F":
                            continue
                        high(st, 2, kind, i)
                        if (kind, i) == ("P", 0) and not is_tail(b, k):
                            nb, nk = (b, k + 1) if k < STEPS - 1 else (b + 1, 0)
                            maps(st, 0, nb, nk)
                            if k == 0 and not first(b):
                                act.wait_ge(s_top, 3 * b - 1)
                                relu_top(h2, 2, bt2).then_inc(s_topr, 1)

            run(act, body)
            maps(Step(BLOCKS - 1, STEPS - 1, True), 2, BLOCKS - 1, STEPS - 1)
            act.wait_ge(s_top, 3 * BLOCKS - 2)
            relu_top(h1, 4, bt1).then_inc(s_topr, 1)
            act.wait_ge(s_top, 3 * BLOCKS - 1)
            relu_top(h2, 2, bt2).then_inc(s_topr, 1)
            act.wait_ge(s_top, 3 * BLOCKS)
            act.wait_ge(s_y, 16 * BLOCKS - 16)
            nc.scalar.activation(y_sb[:, :], misc[0:1, 0:P], ACT.Copy).then_inc(s_topr, 1)

        @block.vector
        def _(dve):
            nc.vector.memset(raw1[HALF:P, TILES - 1, :], 0.0)
            nc.vector.memset(raw2[HALF:P, TILES - 1, :], 0.0).then_inc(s_edge, 1)
            dve.wait_ge(s_sym, 96)
            nc.vector.memset(symB[0:FIELDS, 0, :], 0.0).then_inc(s_edge, 1)
            dve.wait_ge(s_edge, 2)
            nc.vector.tensor_tensor(wF[:ROWS0, 0:3, :], symA[:, 4:7, :], symB[:, 4:7, :], ALU.add)
            nc.vector.tensor_tensor(symA[:, 0:4, :], symA[:, 0:4, :], symB[:, 0:4, :], ALU.add).then_inc(s_added, 1)
            dve.wait_ge(s_wh, 1)
            nc.vector.tensor_tensor(wL[:ROWS0, 0:4, :], symA[:, 0:4, :], wH[:ROWS0, 0:4, :].bitcast(F32),
                                    ALU.subtract).then_inc(s_wl, 1)
            for layer, raw in ((1, raw1), (2, raw2)):
                dve.wait_ge(s_wh, layer + 1)
                t = slice(16 * layer - 12, 16 * layer + 4)
                nc.vector.tensor_tensor(wL[:, t, :], raw[:, 4:TILES, :], wH[:, t, :].bitcast(F32),
                                        ALU.subtract).then_inc(s_wl, 1)

            def multiply(st, layer, pos):
                kind, i = pairs_of(layer)[pos]
                n, rows, tiles = st.n(kind, layer, i), rows_of(layer, pos), tiles_of(layer, pos)
                if layer == 0:
                    x0, xk = rot[:rows, 2 * pos:2 * pos + tiles, :], repP
                else:
                    x0, xk = bc_pair(st, pos), (xk1, xk2)[layer - 1]
                xk = xk[:rows, :].unsqueeze(1).broadcast_to([rows, tiles, CHUNK])
                if kind == "F":
                    wait_count(dve, s_usedF, st.count("F", n + 1 - RF))
                    nc.vector.tensor_tensor(zF[:rows, n % RF, 0:tiles, :], x0, xk, ALU.mult).then_inc(s_mulF, 1)
                elif kind == "P":
                    wait_count(dve, s_loP, st.count("P", n + 1 - RPZ))
                    nc.vector.tensor_tensor(zP[:rows, n % RPZ, 0:tiles, :], x0, xk, ALU.mult).then_inc(s_mulP, 1)
                else:
                    wait_count(dve, s_loD, st.count("D", n))
                    nc.vector.tensor_tensor(zD[:rows, 0:tiles, :], x0, xk, ALU.mult).then_inc(s_mulD, 1)

            def low(st, layer, i):
                n = st.n("D", layer, i)
                dve.wait_ge(s_hiD, st.count("D", n + 1))
                wait_count(dve, s_usedD, st.count("D", n + 1 - RDL))
                nc.vector.tensor_tensor(loD[:, n % RDL, :, :], zD[:, :, :], hiD[:, n % RDH, :, :].bitcast(F32),
                                        ALU.subtract).then_inc(s_loD, 1)

            def layer0(st, c):
                dve.wait_ge(s_rot, 96 * c + 96)
                dve.wait_ge(s_rep, c + 1)
                for pos in range(4):
                    multiply(st, 0, pos)

            layer0(Ahead(), 0)

            def body(b):
                for k in range(STEPS):
                    st = Step(b, k, is_tail(b, k))
                    for layer in (1, 2):
                        dve.wait_ge((s_xk1, s_xk2)[layer - 1], 2 * st.steps() + 2)
                        for pos, (kind, i) in enumerate(PAIRS):
                            if layer == 1 and pos == 0:
                                dve.wait_ge(s_bcA[k % 2], 32 * (2 * b + k // 2 + 1))
                            if layer == 1 and pos in (5, 7):
                                dve.wait_ge(s_bcB[pos // 7], 32 * st.steps() + 32)
                            multiply(st, layer, pos)
                            if kind == "P":
                                low(st, layer, i)
                        if layer == 1 and not is_tail(b, k):
                            layer0(st, st.steps() + 1)

            run(dve, body)

        @block.tensor
        def _(pe):
            pe.wait_ge(s_id, 1)

            def accumulate(st, layer, pos, begin, end):
                kind, i = pairs_of(layer)[pos]
                n, rows, stage_n = st.n(kind, layer, i), rows_of(layer, pos), st.stage(layer)
                dst = acc[:, stage_n % 2, :]
                if begin:
                    wait_count(pe, s_out, 12 * st.b + stage_n - 1)
                terms = []
                if kind == "F":
                    pe.wait_ge(s_mulF, st.count("F", n + 1))
                    for j in range(tiles_of(layer, pos)):
                        w = weight(layer, pos, j)[1]
                        terms.append((wF[:rows, w, :], zF[:rows, n % RF, j, :]))
                else:
                    hi, lo = ((hiP[:, n % RPH], loP[:, n % RPL]) if kind == "P" else
                              (hiD[:, n % RDH], loD[:, n % RDL]))
                    for part in range(2):
                        for j in range(2):
                            w = weight(layer, pos, j)[1]
                            if part == 0:
                                terms.append((wL[:rows, w, :], hi[:rows, j, :]))
                                terms.append((wH[:rows, w, :], hi[:rows, j, :]))
                            else:
                                terms.append((wH[:rows, w, :], lo[:rows, j, :]))
                    pe.wait_ge(s_hiP if kind == "P" else s_hiD, st.count(kind, n + 1))
                for q, (w, z) in enumerate(terms):
                    if kind != "F" and q == 4:
                        pe.wait_ge(s_loP if kind == "P" else s_loD, st.count(kind, n + 1))
                    mm = nc.tensor.matmul(dst, w, z, start=begin and q == 0, stop=end and q == len(terms) - 1)
                mm.then_inc({"F": s_usedF, "P": s_usedP, "D": s_usedD}[kind], 1)

            run_layer0 = [(pos, q == 0, q == 3) for q, pos in enumerate(ORDER0)]

            def transposes(g):
                for j in range(DPC):
                    t = nc.tensor.transpose(misc[:FIELDS, j * P:(j + 1) * P], emb[:, :, DPC * g + j], ident[:, :])
                t.then_inc(s_tr, 1)

            for g in range(STEPS):
                pe.wait_ge(s_gather, 16 * FIELDS)
                wait_count(pe, s_trout, g)
                transposes(g)
            pe.wait_ge(s_wl, 3)
            for pos, begin, end in run_layer0:
                accumulate(Ahead(), 0, pos, begin, end)

            def top1(b):
                pe.wait_ge(s_trout, 5 * b + (9 if not last(b) else 5))
                pe.wait_ge(s_z01, b + 1)
                pe.wait_ge(s_z2, b + 1)
                pe.wait_ge(s_small, 64)
                wait_count(pe, s_topr, 3 * b)
                for m in range(4):
                    cols = slice(m * P, (m + 1) * P)
                    for t in range(2):
                        nc.tensor.matmul(misc[:, cols], wt1[:, t, cols], zsum[:, t, :], start=(t == 0), stop=False)
                    mm = nc.tensor.matmul(misc[:, cols], wt1d[:, cols], denseT[:, :], start=False, stop=True)
                mm.then_inc(s_top, 1)

            def top2(b):
                pe.wait_ge(s_topr, 3 * b + 1)
                for m in range(2):
                    for t in range(4):
                        mm = nc.tensor.matmul(misc[:, m * P:(m + 1) * P], wt2[:, t, m * P:(m + 1) * P], h1[:, t, :],
                                              start=(t == 0), stop=(t == 3))
                mm.then_inc(s_top, 1)

            def top3(b):
                pe.wait_ge(s_topr, 3 * b + 2)
                for t in range(2):
                    mm = nc.tensor.matmul(misc[0:1, 0:P], wt3[:, t:t + 1], h2[:, t, :], start=(t == 0), stop=(t == 1))
                mm.then_inc(s_top, 1)

            def body(b):
                for k in range(STEPS):
                    st = Step(b, k, is_tail(b, k))
                    for q, pos in enumerate(ORDER):
                        group = k == 2 and not last(b) and q in (0, 2, 4, 6)
                        if group and q == 0:
                            pe.wait_ge(s_gather, 16 * FIELDS * b + 2 * 16 * FIELDS)
                            wait_count(pe, s_topr, 3 * b)
                        if group and q > 0:
                            pe.wait_ge(s_trout, 5 * b + 4 + q // 2)
                        accumulate(st, 1, pos, q == 0, q == 9)
                        if group:
                            transposes(q // 2)
                    if k == 0 and not first(b):
                        top1(b - 1)
                    if not is_tail(b, k):
                        for pos, begin, end in run_layer0:
                            accumulate(st, 0, pos, begin, end)
                    if k == 0 and not first(b):
                        top2(b - 1)
                    if k == 2:
                        pe.wait_ge(s_dense, 16 * b + 16)
                        wait_count(pe, s_trout, 5 * b + (4 if last(b) else 8))
                        wait_count(pe, s_topr, 3 * b)
                        nc.tensor.transpose(misc[:D, 0:P], dense[:, :], ident[:, :]).then_inc(s_tr, 1)
                    for q, pos in enumerate(ORDER):
                        accumulate(st, 2, pos, q == 0, q == 9)
                    if k == 0 and not first(b):
                        top3(b - 1)

            run(pe, body)
            top1(BLOCKS - 1)
            top2(BLOCKS - 1)
            top3(BLOCKS - 1)


_TABLES = [f"tbl_{i}" for i in range(FIELDS)]
_WEIGHTS = ["W_top1", "W_top2", "L0_rec_w0", "L0_rec_w1", "L0_rec_w2"]
_COLUMNS = ["L0_rec_b0", "L0_rec_b1", "L0_rec_b2", "b_top1", "b_top2", "W_top3"]


def kernel(**inputs):
    import numpy as np
    import concourse.bacc as bacc
    from concourse.bass_utils import run_bass_kernel_spmd

    nc = bacc.Bacc("TRN2", target_bir_lowering=False, num_devices=1)
    arrays, ins = {}, {}
    columns = np.concatenate([np.asarray(inputs[name]).reshape(-1, P).T for name in _COLUMNS], axis=1)
    for name in ["dense_ctx", "ids", "columns"] + _TABLES + _WEIGHTS:
        a = np.ascontiguousarray(columns if name == "columns" else inputs[name])
        if name == "ids":
            a = np.concatenate([a, a[:P]], axis=0)
        arrays[f"in_{name}"] = a
        ins[name] = nc.dram_tensor(f"in_{name}", a.shape, mybir.dt.from_np(a.dtype), kind="ExternalInput").ap()
    y = nc.dram_tensor("y", (BATCH, 1), F32, kind="ExternalOutput").ap()
    build(nc, ins, y)
    r = run_bass_kernel_spmd(nc, [arrays], core_ids=[0])
    return r.results[0]["y"]
```

```python
from contextlib import ExitStack

import concourse.bass as bass
from concourse import mybir

F32 = mybir.dt.float32
F32R = mybir.dt.float32r
I32 = mybir.dt.int32
ALU = mybir.AluOpType
ACT = mybir.ActivationFunctionType

P = 128
FIELDS = 39
D = 16
BATCH = 2048
HALF = 64
BLOCKS = BATCH // P
CHUNK = 512
DPC = CHUNK // P
STEPS = D // DPC
BCOLS = D * P
PITCH = BATCH * D + 1024
TILES = 20
SHIFTS = 3
TILES0 = 7
ROWS0 = SHIFTS * FIELDS
LAST0 = 2 * FIELDS

PAIRS = [("F", 0), ("P", 0), ("D", 0), ("P", 1), ("D", 1), ("P", 2), ("D", 2), ("P", 3), ("D", 3), ("F", 1)]
PAIRS0 = [("P", 0), ("F", 0), ("P", 1), ("F", 1)]
LOW_AFTER = {3: 0, 5: 1, 7: 2, 9: 3}
ORDER = [("h", 0), ("h", 1), ("h", 2), ("l", 2), ("l", 1), ("h", 3), ("h", 4), ("l", 4), ("l", 3), ("h", 5), ("h", 6),
         ("l", 6), ("l", 5), ("h", 7), ("h", 8), ("h", 9), ("l", 8), ("l", 7)]
GROUPS = [("l", 2), ("l", 1), ("l", 4), ("l", 3)]
ORDER0 = [("h", 1), ("h", 0), ("h", 3), ("h", 2), ("l", 0), ("l", 2)]
PER_STEP = {"F": 6, "D": 8, "P": 10}
AHEAD = {"F": 2, "D": 0, "P": 2}
BEFORE = {
    "F": {1: 0, 0: 2, 2: 4},
    "D": {1: 0, 0: 4, 2: 4},
    "P": {1: 0, 0: 4, 2: 6},
}
RF, RPZ, RPH, RPL, RDH, RDL = 3, 2, 4, 2, 2, 2
DOUBLE = 5
LATE_SLOTS, EARLY_FROM = 23, 28
EARLY = 14


def build(nc, ins, y_out):
    x0_dram = nc.dram_tensor("x0_scratch", [2 * FIELDS, PITCH], F32).ap()
    w0c_dram = nc.dram_tensor("w0_columns_twice", [FIELDS, 2 * FIELDS, P], F32).ap()
    w0r_dram = nc.dram_tensor("w0_rows_twice", [2 * FIELDS, FIELDS, P], F32).ap()

    with ExitStack() as ctx:
        def sb(name, shape, dt=F32):
            return ctx.enter_context(nc.sbuf_tensor(name, shape, dt))

        def ps(name, shape):
            return ctx.enter_context(nc.psum_tensor(name, shape, F32))

        def sem(name):
            return ctx.enter_context(nc.semaphore(name))

        bcA = sb("bcA", [P, 2, 2 * DOUBLE, CHUNK])
        bcB = sb("bcB", [P, TILES - 2 * DOUBLE, CHUNK])
        rot = sb("rot", [ROWS0, TILES0, CHUNK])
        rep = sb("rep", [ROWS0, CHUNK])
        zF = sb("zF", [P, RF, 2, CHUNK])
        zP = sb("zP", [P, RPZ, 2, CHUNK])
        hiP = sb("hiP", [P, RPH, 2, CHUNK], F32R)
        loP = sb("loP", [P, RPL, 2, CHUNK], F32R)
        hiD = sb("hiD", [P, RDH, 2, CHUNK], F32R)
        loD = sb("loD", [P, RDL, 2, CHUNK], F32R)
        n_f, n_r = 3 + 4 + 4, 4 + 16 + 16
        wF = sb("wF", [P, n_f, P])
        wH = sb("wH", [P, n_r, P], F32R)
        wL = sb("wL", [P, n_r, P], F32R)
        columns = sb("columns", [P, 11])
        bias, bt1, bt2, wt3 = columns[:, 0:3], columns[:, 3:7], columns[:, 7:9], columns[:, 9:11]
        ids_sb = sb("ids_sb", [P, FIELDS], I32)
        emb = sb("emb", [P, FIELDS, D])
        dense = sb("dense", [P, D])
        ident = sb("ident", [P, P])
        x0T = sb("x0T", [FIELDS, 2, CHUNK])
        denseT = sb("denseT", [D, P])
        sum01 = sb("sum01", [P, CHUNK])
        sum2 = sb("sum2", [P, CHUNK])
        dir01 = sb("dir01", [P, CHUNK])
        dir2 = sb("dir2", [P, CHUNK])
        zsum = sb("zsum", [P, 2, P])
        wt1 = sb("wt1", [P, 2, 512])
        wt1d = sb("wt1d", [D, 512])
        wt2 = sb("wt2", [P, 4, 256])
        h1 = sb("h1", [P, 4, P])
        h2 = sb("h2", [P, 2, P])
        y_sb = sb("y_sb", [1, P])

        acc = ps("acc", [P, 2, CHUNK])
        xk1 = ps("xk1", [P, CHUNK])
        xk2 = ps("xk2", [P, CHUNK])
        repP = ps("repP", [P, CHUNK])
        zD = ps("zD", [P, 2, CHUNK])
        misc = ps("misc", [P, CHUNK])

        stage = bcA[:, :, :, :].rearrange("p a t n -> p (a t n)")
        raw1 = stage[:, 0:TILES * P].rearrange("p (t s) -> p t s", s=P)
        raw2 = stage[:, TILES * P:2 * TILES * P].rearrange("p (t s) -> p t s", s=P)
        o = 2 * TILES * P
        symA = stage[:ROWS0, o:o + TILES0 * P].rearrange("p (t s) -> p t s", s=P)
        symB = stage[:ROWS0, o + TILES0 * P:o + 2 * TILES0 * P].rearrange("p (t s) -> p t s", s=P)

        s_w0c = sem("s_w0_columns_twice")
        s_w0r = sem("s_w0_rows_twice")
        s_sym = sem("s_sym_in")
        s_raw = sem("s_raw_in")
        s_small = sem("s_small_in")
        s_edge = sem("s_edge_zeroed")
        s_added = sem("s_sym_added")
        s_wh = sem("s_weights_hi")
        s_wl = sem("s_weights_split")
        s_id0 = sem("s_ident_zeroed")
        s_id = sem("s_ident_ready")
        s_ids = sem("s_ids_in")
        s_gather = sem("s_gathered")
        s_tr = sem("s_transposed")
        s_trout = sem("s_transposes_read")
        s_x0w = [sem(f"s_x0_written{g}") for g in range(STEPS)]
        s_dense = sem("s_dense_in")
        s_rot = sem("s_rot_in")
        s_rep = sem("s_rep_in_psum")
        s_bcA = [sem(f"s_bcA_in{p}") for p in range(2)]
        s_bcB = [sem(f"s_bcB_in{p}") for p in range(2)]
        s_mulF = sem("s_mulF")
        s_mulP = sem("s_mulP")
        s_mulD = sem("s_mulD")
        s_hiP = sem("s_hiP")
        s_hiD = sem("s_hiD")
        s_loP = sem("s_loP")
        s_loD = sem("s_loD")
        s_usedF = sem("s_usedF")
        s_usedP = sem("s_usedP")
        s_usedD = sem("s_usedD")
        s_out = sem("s_acc_read")
        s_xk1 = sem("s_xk1_ready")
        s_xk2 = sem("s_xk2_ready")
        s_add01 = sem("s_dir01_added")
        s_add2 = sem("s_dir2_added")
        s_half01 = sem("s_sum01_halved")
        s_half2 = sem("s_sum2_halved")
        s_z01 = sem("s_zsum01_ready")
        s_z2 = sem("s_zsum2_ready")
        s_top = sem("s_top_psum")
        s_topr = sem("s_top_read")
        s_y = sem("s_y_out")

        class Step:

            def __init__(self, b, k, tail=False):
                self.b, self.k, self.tail = b, k, tail

            def n(self, kind, layer, i):
                cut = AHEAD[kind] if self.tail and layer == 2 else 0
                return AHEAD[kind] + PER_STEP[kind] * self.k + BEFORE[kind][layer] + i - cut

            def count(self, kind, local):
                return PER_STEP[kind] * STEPS * self.b + local

            def stage(self, layer):
                return 1 + 3 * self.k + {1: 0, 0: 1, 2: 2}[layer] - (1 if self.tail and layer == 2 else 0)

            def steps(self):
                return self.b * STEPS + self.k

        class Ahead(Step):

            def __init__(self):
                super().__init__(0, 0)

            def n(self, kind, layer, i):
                return i

            def stage(self, layer):
                return 0

            def steps(self):
                return -1

        def wait_count(eng, s, value):
            if isinstance(value, int) and value <= 0:
                return
            eng.wait_ge(s, value)

        def multiplied(st, layer, pos):
            kind, i = pairs_of(layer)[pos]
            return {"F": s_mulF, "D": s_mulD, "P": s_mulP}[kind], st.count(kind, st.n(kind, layer, i) + 1)

        def in_registers(eng, *values):
            return [v if isinstance(v, int) else eng.to_reg(v) for v in values]

        def pairs_of(layer):
            return PAIRS0 if layer == 0 else PAIRS

        def tiles_of(layer, pos):
            return 1 if layer == 0 and pos == 3 else 2

        def rows_of(layer, pos):
            return P if layer else (LAST0 if pos == 3 else ROWS0)

        def bc_pair(st, pos):
            if pos < DOUBLE:
                return bcA[:, st.k % 2, 2 * pos:2 * pos + 2, :]
            q = pos - DOUBLE
            return bcB[:, 2 * q:2 * q + 2, :]

        def weight(layer, pos, j):
            kind, i = pairs_of(layer)[pos]
            if kind == "F":
                return kind, {0: 0, 1: 3, 2: 7}[layer] + 2 * i + j
            before = sum(x != "F" for x, _ in pairs_of(layer)[:pos])
            return kind, {0: 0, 1: 4, 2: 20}[layer] + 2 * before + j

        def weights_of(layer):
            rows = P if layer else ROWS0
            raw = (symA, raw1, raw2)[layer]
            for pos in range(len(pairs_of(layer))):
                kind, w = weight(layer, pos, 0)
                tiles = tiles_of(layer, pos)
                yield kind, raw[:, 2 * pos:2 * pos + tiles, :], slice(w, w + tiles), rows

        def run(engine, body):
            body(0)
            with engine.Fori(1, BLOCKS - 1) as b:
                body(b)
            body(BLOCKS - 1)

        def first(b):
            return isinstance(b, int) and b == 0

        def last(b):
            return isinstance(b, int) and b == BLOCKS - 1

        def is_tail(b, k):
            return last(b) and k == STEPS - 1

        block = ctx.enter_context(nc.Block())

        @block.sync
        def _(sp):
            def load_ids(b):
                sp.dma_start(ids_sb[:, :], ins["ids"][bass.ds(b * P, P), :]).then_inc(s_ids, 16)

            def load_dense(b):
                sp.dma_start(dense[:, :], ins["dense_ctx"][bass.ds(b * P, P), :]).then_inc(s_dense, 16)

            def x0_rows(row, col, dims):
                return bass.AP(tensor=x0_dram.tensor, offset=col + row * PITCH, ap=dims)

            def load_rot(b, k):
                col = b * BCOLS + k * CHUNK
                for j in range(SHIFTS):
                    sp.dma_start(rot[j * FIELDS:(j + 1) * FIELDS, :, :],
                                 x0_rows(j, col, [[PITCH, FIELDS], [SHIFTS * PITCH, TILES0], [1, CHUNK]])
                                 ).then_inc(s_rot, 16)
                for j in range(SHIFTS):
                    sp.dma_start(rep[j * FIELDS:(j + 1) * FIELDS, :],
                                 x0_rows(0, col, [[PITCH, FIELDS], [1, CHUNK]])).then_inc(s_rot, 16)

            def load_bcA(b, k):
                col = b * BCOLS + k * CHUNK
                for h in range(2):
                    sp.dma_start(bcA[h * HALF:(h + 1) * HALF, k % 2, :, :],
                                 x0_rows(h, col, [[0, HALF], [2 * PITCH, 2 * DOUBLE], [1, CHUNK]])
                                 ).then_inc(s_bcA[k % 2], 16)

            def load_bcB(b, k, part):
                lo, hi = [(DOUBLE, 7), (7, 10)][part]
                col = b * BCOLS + k * CHUNK
                for h in range(2):
                    sp.dma_start(bcB[h * HALF:(h + 1) * HALF, 2 * (lo - DOUBLE):2 * (hi - DOUBLE), :],
                                 x0_rows(4 * lo + h, col, [[0, HALF], [2 * PITCH, 2 * (hi - lo)], [1, CHUNK]])
                                 ).then_inc(s_bcB[part], 16)

            def write_x0(b, g):
                col = b * BCOLS + g * CHUNK
                for twice in range(2):
                    sp.dma_start(x0_dram[twice * FIELDS:(twice + 1) * FIELDS, bass.ds(col, CHUNK)],
                                 x0T[:, g % 2, :]).then_inc(s_x0w[g], 16)

            load_ids(0)
            w0 = ins["L0_rec_w0"]
            for twice in range(2):
                sp.dma_start(w0c_dram[:, twice * FIELDS:(twice + 1) * FIELDS, :], w0).then_inc(s_w0c, 16)
                sp.dma_start(w0r_dram[twice * FIELDS:(twice + 1) * FIELDS, :, :], w0).then_inc(s_w0r, 16)
            for layer, raw in ((1, raw1), (2, raw2)):
                w = ins[f"L0_rec_w{layer}"].rearrange("h k s -> (h k) s")
                sp.dma_start(raw[:, 0:TILES - 1, :],
                             w[0:(TILES - 1) * P, :].rearrange("(t p) s -> p t s", p=P)).then_inc(s_raw, 16)
                sp.dma_start(raw[0:HALF, TILES - 1, :], w[(TILES - 1) * P:FIELDS * HALF, :]).then_inc(s_raw, 16)
            sp.wait_ge(s_w0c, 32)
            sp.wait_ge(s_w0r, 32)
            for j in range(SHIFTS):
                sp.dma_start(symA[j * FIELDS:(j + 1) * FIELDS, :, :],
                             bass.AP(tensor=w0c_dram.tensor, offset=j * P,
                                     ap=[[(2 * FIELDS + 1) * P, FIELDS], [SHIFTS * P, TILES0], [1, P]])
                             ).then_inc(s_sym, 16)
                sp.dma_start(symB[j * FIELDS:(j + 1) * FIELDS, :, :],
                             bass.AP(tensor=w0r_dram.tensor, offset=j * FIELDS * P,
                                     ap=[[(FIELDS + 1) * P, FIELDS], [SHIFTS * FIELDS * P, TILES0], [1, P]])
                             ).then_inc(s_sym, 16)
            sp.dma_start(columns[:, :], ins["columns"]).then_inc(s_small, 16)
            sp.dma_start(wt1[:, :, :], ins["W_top1"][0:2 * P, :].rearrange("(t p) n -> p t n", p=P)).then_inc(s_small, 16)
            sp.dma_start(wt1d[:, :], ins["W_top1"][2 * P:2 * P + D, :]).then_inc(s_small, 16)
            sp.dma_start(wt2[:, :, :], ins["W_top2"].rearrange("(t p) n -> p t n", p=P)).then_inc(s_small, 16)

            for g in range(STEPS):
                sp.wait_ge(s_trout, g + 1)
                write_x0(0, g)
                if g == 0:
                    sp.wait_ge(s_x0w[0], 32)
                    load_rot(0, 0)
            sp.wait_ge(s_gather, 16 * FIELDS)
            load_ids(1)
            sp.wait_ge(s_wl, 3)
            load_bcA(0, 0)
            load_bcB(0, 0, 0)
            load_bcB(0, 0, 1)
            sp.wait_ge(s_mulF, 2)
            sp.wait_ge(s_x0w[1], 32)
            load_rot(0, 1)

            def body(b):
                for k in range(STEPS):
                    st = Step(b, k, is_tail(b, k))
                    nb, nk = (b, k + 1) if k < STEPS - 1 else (b + 1, 0)
                    rb, rk = (b, k + 2) if k < STEPS - 2 else (b + 1, k - 2)
                    if not is_tail(b, k):
                        s, v = multiplied(st, 2, DOUBLE - 1)
                        used, written = in_registers(sp, v - PER_STEP[PAIRS[DOUBLE - 1][0]], 32 * nb + 32)
                        wait_count(sp, s, used)
                        sp.wait_ge(s_x0w[nk], written)
                        load_bcA(nb, nk)
                    if k == 0:
                        wait_count(sp, s_tr, 5 * b + 4)
                        load_dense(b)
                    if k == 1 and not first(b):
                        sp.wait_ge(s_topr, 3 * b)
                        sp.dma_start(y_out[bass.ds(b * P - P, P), :].rearrange("n a -> a n"), y_sb[:, :]).then_inc(s_y, 16)
                    if k == 2 and not last(b):
                        sp.wait_ge(s_gather, (16 * FIELDS) * b + 2 * 16 * FIELDS)
                        load_ids(b + 2)
                        for g in range(STEPS - 1):
                            sp.wait_ge(s_trout, 5 * b + 6 + g)
                            write_x0(b + 1, g)
                    if k == 2 and not last(b):
                        sp.wait_ge(*multiplied(st, 2, 6))
                        load_bcB(nb, nk, 0)
                        sp.wait_ge(s_trout, 5 * b + 9)
                        write_x0(b + 1, STEPS - 1)
                    if not (last(b) and k >= STEPS - 2):
                        used, written = in_registers(sp, st.count("F", st.n("F", 0, 1) + 1), 32 * rb + 32)
                        sp.wait_ge(s_mulF, used)
                        sp.wait_ge(s_x0w[rk], written)
                        load_rot(rb, rk)
                    if not is_tail(b, k):
                        if k != 2 or last(b):
                            sp.wait_ge(*multiplied(st, 2, 6))
                            load_bcB(nb, nk, 0)
                        sp.wait_ge(*multiplied(st, 2, 9))
                        load_bcB(nb, nk, 1)

            run(sp, body)
            sp.wait_ge(s_topr, 3 * BLOCKS)
            sp.dma_start(y_out[BATCH - P:BATCH, :].rearrange("n a -> a n"), y_sb[:, :]).then_inc(s_y, 16)
            sp.wait_ge(s_y, 16 * BLOCKS)

        @block.gpsimd
        def _(pool):
            nc.gpsimd.memset(ident[:, :], 0.0).then_inc(s_id0, 1)
            pool.wait_ge(s_id0, 1)
            nc.gpsimd.affine_select(out=ident[:, :], in_=ident[:, :], compare_op=ALU.not_equal, fill=1.0, base=0,
                                    pattern=[[-1, P]], channel_multiplier=1).then_inc(s_id, 1)

            def gather(field):
                pool.indirect_dma_start(emb[:, field, :], None, ins[f"tbl_{field}"][:, :],
                                        bass.IndirectOffsetOnAxis(ap=ids_sb[:, field:field + 1], axis=0)
                                        ).then_inc(s_gather, 16)

            def low(st, layer, i):
                n = st.n("P", layer, i)
                rows = P if layer else ROWS0
                pool.wait_ge(s_hiP, st.count("P", n + 1))
                wait_count(pool, s_usedP, st.count("P", n + 1 - RPL))
                nc.gpsimd.tensor_tensor(loP[:rows, n % RPL, :, :], zP[:rows, n % RPZ, :, :],
                                        hiP[:rows, n % RPH, :, :].bitcast(F32), ALU.subtract).then_inc(s_loP, 1)

            def finish2(b):
                pool.wait_ge(s_out, 12 * b + 13 - (1 if last(b) else 0))
                pool.wait_ge(s_add2, 3 * b + 2)
                nc.gpsimd.tensor_tensor(sum2[:, :], sum2[:, :], dir2[:, :], ALU.add).then_inc(s_add2, 1)
                pool.wait_ge(s_add2, 3 * b + 3)
                nc.gpsimd.tensor_tensor(sum2[:, 0:2 * P], sum2[:, 0:2 * P], sum2[:, 2 * P:4 * P],
                                        ALU.add).then_inc(s_half2, 1)
                pool.wait_ge(s_half2, b + 1)
                nc.gpsimd.tensor_tensor(zsum[:, 1, :], sum2[:, 0:P], sum2[:, P:2 * P], ALU.add).then_inc(s_z2, 1)

            pool.wait_ge(s_ids, 16)
            for f in range(FIELDS):
                gather(f)
            for i in range(2):
                low(Ahead(), 0, i)

            def body(b):
                late = [] if last(b) else list(range(0 if first(b) else EARLY, FIELDS))
                early = [] if last(b) else list(range(EARLY))

                def gathers(k, s):
                    slot = s + 10 * k
                    todo, q, slots = (late, slot, LATE_SLOTS) if slot < EARLY_FROM else (early, slot - EARLY_FROM,
                                                                                        10 * STEPS - EARLY_FROM)
                    fields = todo[q * len(todo) // slots:(q + 1) * len(todo) // slots] if q < slots else []
                    if first(b) and k == 0 and s == 0:
                        pool.wait_ge(s_ids, 32)
                        pool.wait_ge(s_tr, 4)
                    for f in fields:
                        gather(f)

                for k in range(STEPS):
                    st = Step(b, k, is_tail(b, k))
                    for i in range(4):
                        low(st, 1, i)
                        gathers(k, i)
                        if i == 1 and k == 0 and not first(b):
                            finish2(b - 1)
                        if i == 1 and k >= 2:
                            pool.wait_ge(s_out, 12 * b + st.stage(1))
                            pool.wait_ge(s_add2, 3 * b + k - 2) if k == 3 else wait_count(pool, s_add2, 3 * b)
                            nc.gpsimd.tensor_tensor(sum2[:, :], sum2[:, :], dir2[:, :], ALU.add).then_inc(s_add2, 1)
                    if not is_tail(b, k):
                        for i in range(2):
                            low(st, 0, i)
                            gathers(k, 4 + i)
                    if k > 0:
                        pool.wait_ge(s_out, 12 * b + st.stage(1) + 1)
                        wait_count(pool, s_add01, 3 * b + k - 1)
                        nc.gpsimd.tensor_tensor(sum01[:, :], sum01[:, :], dir01[:, :], ALU.add).then_inc(s_add01, 1)
                    if k == STEPS - 1:
                        pool.wait_ge(s_add01, 3 * b + 3)
                        nc.gpsimd.tensor_tensor(sum01[:, 0:2 * P], sum01[:, 0:2 * P], sum01[:, 2 * P:4 * P],
                                                ALU.add).then_inc(s_half01, 1)
                        pool.wait_ge(s_half01, b + 1)
                        nc.gpsimd.tensor_tensor(zsum[:, 0, :], sum01[:, 0:P], sum01[:, P:2 * P],
                                                ALU.add).then_inc(s_z01, 1)
                    for i in range(4):
                        if 10 * k + 6 + i == EARLY_FROM and not last(b):
                            pool.wait_ge(s_ids, 16 * b + 48)
                            pool.wait_ge(s_tr, 5 * b + 9)
                        low(st, 2, i)
                        gathers(k, 6 + i)

            run(pool, body)
            finish2(BLOCKS - 1)

        @block.scalar
        def _(act):
            act.wait_ge(s_added, 1)
            def split_weights(layer):
                for kind, raw, w, rows in weights_of(layer):
                    dst = (wF if kind == "F" else wH)[:rows, w, :]
                    a = nc.scalar.activation(dst, raw, ACT.Copy)
                a.then_inc(s_wh, 1)

            split_weights(0)
            act.wait_ge(s_raw, 64)
            act.wait_ge(s_edge, 1)
            split_weights(1)
            split_weights(2)

            def high(st, layer, kind, i):
                n = st.n(kind, layer, i)
                rows = P if layer else ROWS0
                if kind == "P":
                    act.wait_ge(s_mulP, st.count("P", n + 1))
                    wait_count(act, s_usedP, st.count("P", n + 1 - RPH))
                    nc.scalar.activation(hiP[:rows, n % RPH, :, :], zP[:rows, n % RPZ, :, :],
                                         ACT.Copy).then_inc(s_hiP, 1)
                else:
                    act.wait_ge(s_mulD, st.count("D", n + 1))
                    wait_count(act, s_usedD, st.count("D", n + 1 - RDH))
                    nc.scalar.activation(hiD[:, n % RDH, :, :], zD[:, :, :], ACT.Copy).then_inc(s_hiD, 1)

            def maps(st, layer, b, k):
                n = st.stage(layer)
                kind, i = pairs_of(layer)[(ORDER if layer else ORDER0)[-1][1]]
                act.wait_ge({"F": s_usedF, "D": s_usedD, "P": s_usedP}[kind], st.count(kind, st.n(kind, layer, i) + 1))
                src = acc[:, n % 2, :]
                if layer < 2:
                    xk, ready = ((xk1, s_xk1), (xk2, s_xk2))[layer]
                    for h in range(2):
                        nc.scalar.activation(xk[h * HALF:(h + 1) * HALF, :], src[0:HALF, :], ACT.Relu,
                                             bias=bias[0:HALF, layer:layer + 1]).then_inc(ready, 1)
                    wait_count(act, s_z01, b) if k == 0 else wait_count(act, s_add01, 3 * b + k - 1)
                    dst = sum01 if k == 0 else dir01
                    nc.scalar.activation(dst[layer * HALF:(layer + 1) * HALF, :], src[HALF:P, :], ACT.Relu,
                                         bias=bias[HALF:P, layer:layer + 1]).then_inc(s_out, 1)
                else:
                    wait_count(act, s_z2, b) if k == 0 else wait_count(act, s_add2, 3 * b + k - 1)
                    dst = sum2 if k == 0 else dir2
                    nc.scalar.activation(dst[:, :], src, ACT.Relu, bias=bias[:, 2:3]).then_inc(s_out, 1)

            def rep_to_psum(c):
                act.wait_ge(s_rot, 96 * c + 96)
                nc.scalar.activation(repP[:ROWS0, :], rep[:, :], ACT.Copy).then_inc(s_rep, 1)

            def transposed(b, g, n):
                act.wait_ge(s_tr, n)
                wait_count(act, s_x0w[(g - 2) % STEPS], 32 * b + (32 if g >= 2 else 0))
                nc.scalar.activation(x0T[:, g % 2, :], misc[:FIELDS, :], ACT.Copy).then_inc(s_trout, 1)

            for g in range(STEPS):
                transposed(0, g, g + 1)
            rep_to_psum(0)
            act.wait_ge(s_small, 64)
            for i in range(2):
                high(Ahead(), 0, "P", i)
            maps(Ahead(), 0, 0, 0)

            def relu_top(dst, n, b_col):
                for m in range(n):
                    a = nc.scalar.activation(dst[:, m, :], misc[:, m * P:(m + 1) * P], ACT.Relu,
                                             bias=b_col[:, m:m + 1])
                return a

            def body(b):
                for k in range(STEPS):
                    st = Step(b, k, is_tail(b, k))
                    for pos, (kind, i) in enumerate(PAIRS):
                        if kind == "F":
                            continue
                        high(st, 1, kind, i)
                        if (kind, i) == ("D", 1) and not (first(b) and k == 0):
                            before = Step(b, k - 1) if k else Step(b - 1, STEPS - 1)
                            maps(before, 2, before.b, before.k)
                        if (kind, i) == ("D", 1) and k == 1 and not first(b):
                            act.wait_ge(s_top, 3 * b)
                            wait_count(act, s_y, 16 * b - 16)
                            nc.scalar.activation(y_sb[:, :], misc[0:1, 0:P], ACT.Copy).then_inc(s_topr, 1)
                        if (kind, i) == ("P", 1) and not is_tail(b, k):
                            rep_to_psum(st.steps() + 1)
                    if not is_tail(b, k):
                        high(st, 0, "P", 0)
                    maps(st, 1, b, k)
                    if not is_tail(b, k):
                        high(st, 0, "P", 1)
                    if k == 0 and not first(b):
                        act.wait_ge(s_top, 3 * b - 2)
                        relu_top(h1, 4, bt1).then_inc(s_topr, 1)
                    if k == 2:
                        act.wait_ge(s_tr, 5 * b + 5)
                        wait_count(act, s_top, 3 * b - 2)
                        nc.scalar.activation(denseT[:, :], misc[:D, 0:P], ACT.Copy).then_inc(s_trout, 1)
                    for pos, (kind, i) in enumerate(PAIRS):
                        if kind == "F":
                            continue
                        high(st, 2, kind, i)
                        if kind == "D" and k == 2 and not last(b):
                            transposed(b + 1, i, 5 * b + 6 + i)
                        if (kind, i) == ("P", 2) and not is_tail(b, k):
                            nb, nk = (b, k + 1) if k < STEPS - 1 else (b + 1, 0)
                            maps(st, 0, nb, nk)
                            if k == 0 and not first(b):
                                act.wait_ge(s_top, 3 * b - 1)
                                relu_top(h2, 2, bt2).then_inc(s_topr, 1)

            run(act, body)
            maps(Step(BLOCKS - 1, STEPS - 1, True), 2, BLOCKS - 1, STEPS - 1)
            act.wait_ge(s_top, 3 * BLOCKS - 2)
            relu_top(h1, 4, bt1).then_inc(s_topr, 1)
            act.wait_ge(s_top, 3 * BLOCKS - 1)
            relu_top(h2, 2, bt2).then_inc(s_topr, 1)
            act.wait_ge(s_top, 3 * BLOCKS)
            act.wait_ge(s_y, 16 * BLOCKS - 16)
            nc.scalar.activation(y_sb[:, :], misc[0:1, 0:P], ACT.Copy).then_inc(s_topr, 1)

        @block.vector
        def _(dve):
            nc.vector.memset(raw1[HALF:P, TILES - 1, :], 0.0)
            nc.vector.memset(raw2[HALF:P, TILES - 1, :], 0.0).then_inc(s_edge, 1)
            dve.wait_ge(s_sym, 96)
            nc.vector.memset(symB[0:FIELDS, 0, :], 0.0).then_inc(s_edge, 1)
            dve.wait_ge(s_edge, 2)
            nc.vector.tensor_tensor(symA[:, :, :], symA[:, :, :], symB[:, :, :], ALU.add).then_inc(s_added, 1)
            for layer in range(3):
                dve.wait_ge(s_wh, layer + 1)
                for kind, raw, w, rows in weights_of(layer):
                    if kind != "F":
                        a = nc.vector.tensor_tensor(wL[:rows, w, :], raw, wH[:rows, w, :].bitcast(F32), ALU.subtract)
                a.then_inc(s_wl, 1)

            def multiply(st, layer, pos):
                kind, i = pairs_of(layer)[pos]
                n, rows, tiles = st.n(kind, layer, i), rows_of(layer, pos), tiles_of(layer, pos)
                if layer == 0:
                    x0, xk = rot[:rows, 2 * pos:2 * pos + tiles, :], repP
                else:
                    x0, xk = bc_pair(st, pos), (xk1, xk2)[layer - 1]
                xk = xk[:rows, :].unsqueeze(1).broadcast_to([rows, tiles, CHUNK])
                if kind == "F":
                    wait_count(dve, s_usedF, st.count("F", n + 1 - RF))
                    nc.vector.tensor_tensor(zF[:rows, n % RF, 0:tiles, :], x0, xk, ALU.mult).then_inc(s_mulF, 1)
                elif kind == "P":
                    wait_count(dve, s_loP, st.count("P", n + 1 - RPZ))
                    nc.vector.tensor_tensor(zP[:rows, n % RPZ, 0:tiles, :], x0, xk, ALU.mult).then_inc(s_mulP, 1)
                else:
                    wait_count(dve, s_loD, st.count("D", n))
                    nc.vector.tensor_tensor(zD[:rows, 0:tiles, :], x0, xk, ALU.mult).then_inc(s_mulD, 1)

            def low(st, layer, i):
                n = st.n("D", layer, i)
                dve.wait_ge(s_hiD, st.count("D", n + 1))
                wait_count(dve, s_usedD, st.count("D", n + 1 - RDL))
                nc.vector.tensor_tensor(loD[:, n % RDL, :, :], zD[:, :, :], hiD[:, n % RDH, :, :].bitcast(F32),
                                        ALU.subtract).then_inc(s_loD, 1)

            def layer0(st, c):
                dve.wait_ge(s_rot, 96 * c + 96)
                dve.wait_ge(s_rep, c + 1)
                for pos in range(4):
                    multiply(st, 0, pos)

            layer0(Ahead(), 0)

            def body(b):
                for k in range(STEPS):
                    st = Step(b, k, is_tail(b, k))
                    for layer in (1, 2):
                        dve.wait_ge((s_xk1, s_xk2)[layer - 1], 2 * st.steps() + 2)
                        for pos, (kind, i) in enumerate(PAIRS):
                            if layer == 1 and pos == 0:
                                dve.wait_ge(s_bcA[k % 2], 32 * (2 * b + k // 2 + 1))
                            if layer == 1 and pos in (5, 7):
                                dve.wait_ge(s_bcB[pos // 7], 32 * st.steps() + 32)
                            multiply(st, layer, pos)
                            if pos in LOW_AFTER:
                                low(st, layer, LOW_AFTER[pos])
                        if layer == 1 and not is_tail(b, k):
                            layer0(st, st.steps() + 1)

            run(dve, body)

        @block.tensor
        def _(pe):
            pe.wait_ge(s_id, 1)

            def accumulate(st, layer, q):
                order = ORDER if layer else ORDER0
                part, pos = order[q]
                kind, i = pairs_of(layer)[pos]
                n, rows, stage_n = st.n(kind, layer, i), rows_of(layer, pos), st.stage(layer)
                begin, end = q == 0, q == len(order) - 1
                if begin:
                    wait_count(pe, s_out, 12 * st.b + stage_n - 1)
                if kind == "F":
                    z, ready, used, weights = zF[:rows, n % RF], s_mulF, s_usedF, [wF]
                elif kind == "P":
                    z = hiP[:rows, n % RPH] if part == "h" else loP[:rows, n % RPL]
                    ready, used = (s_hiP if part == "h" else s_loP), s_usedP
                else:
                    z = hiD[:rows, n % RDH] if part == "h" else loD[:rows, n % RDL]
                    ready, used = (s_hiD if part == "h" else s_loD), s_usedD
                if kind != "F":
                    weights = [wL, wH] if part == "h" else [wH]
                pe.wait_ge(ready, st.count(kind, n + 1))
                terms = [(x[:rows, weight(layer, pos, j)[1], :], z[:, j, :])
                         for j in range(tiles_of(layer, pos)) for x in weights]
                for t, (w, x) in enumerate(terms):
                    mm = nc.tensor.matmul(acc[:, stage_n % 2, :], w, x, start=begin and t == 0,
                                          stop=end and t == len(terms) - 1)
                if kind == "F" or part == "l":
                    mm.then_inc(used, 1)

            def run_layer0(st):
                for q in range(len(ORDER0)):
                    accumulate(st, 0, q)

            def transposes(g):
                for j in range(DPC):
                    t = nc.tensor.transpose(misc[:FIELDS, j * P:(j + 1) * P], emb[:, :, DPC * g + j], ident[:, :])
                t.then_inc(s_tr, 1)

            for g in range(STEPS):
                pe.wait_ge(s_gather, 16 * FIELDS)
                wait_count(pe, s_trout, g)
                transposes(g)
            pe.wait_ge(s_wl, 3)
            run_layer0(Ahead())

            def top1(b):
                pe.wait_ge(s_trout, 5 * b + (9 if not last(b) else 5))
                pe.wait_ge(s_z01, b + 1)
                pe.wait_ge(s_z2, b + 1)
                pe.wait_ge(s_small, 64)
                wait_count(pe, s_topr, 3 * b)
                for m in range(4):
                    cols = slice(m * P, (m + 1) * P)
                    for t in range(2):
                        nc.tensor.matmul(misc[:, cols], wt1[:, t, cols], zsum[:, t, :], start=(t == 0), stop=False)
                    mm = nc.tensor.matmul(misc[:, cols], wt1d[:, cols], denseT[:, :], start=False, stop=True)
                mm.then_inc(s_top, 1)

            def top2(b):
                pe.wait_ge(s_topr, 3 * b + 1)
                for m in range(2):
                    for t in range(4):
                        mm = nc.tensor.matmul(misc[:, m * P:(m + 1) * P], wt2[:, t, m * P:(m + 1) * P], h1[:, t, :],
                                              start=(t == 0), stop=(t == 3))
                mm.then_inc(s_top, 1)

            def top3(b):
                pe.wait_ge(s_topr, 3 * b + 2)
                for t in range(2):
                    mm = nc.tensor.matmul(misc[0:1, 0:P], wt3[:, t:t + 1], h2[:, t, :], start=(t == 0), stop=(t == 1))
                mm.then_inc(s_top, 1)

            def body(b):
                for k in range(STEPS):
                    st = Step(b, k, is_tail(b, k))
                    for q in range(len(ORDER)):
                        accumulate(st, 1, q)
                    if k == 0 and not first(b):
                        top1(b - 1)
                    if not is_tail(b, k):
                        run_layer0(st)
                    if k == 0 and not first(b):
                        top2(b - 1)
                    if k == 2:
                        pe.wait_ge(s_dense, 16 * b + 16)
                        wait_count(pe, s_trout, 5 * b + 4)
                        wait_count(pe, s_topr, 3 * b)
                        nc.tensor.transpose(misc[:D, 0:P], dense[:, :], ident[:, :]).then_inc(s_tr, 1)
                    for q in range(len(ORDER)):
                        group = k == 2 and not last(b) and ORDER[q] in GROUPS
                        if group:
                            g = GROUPS.index(ORDER[q])
                            if g == 0:
                                pe.wait_ge(s_gather, 16 * FIELDS * b + 2 * 16 * FIELDS)
                            pe.wait_ge(s_trout, 5 * b + 5 + g)
                        accumulate(st, 2, q)
                        if group:
                            transposes(g)
                    if k == 0 and not first(b):
                        top3(b - 1)

            run(pe, body)
            top1(BLOCKS - 1)
            top2(BLOCKS - 1)
            top3(BLOCKS - 1)


_TABLES = [f"tbl_{i}" for i in range(FIELDS)]
_WEIGHTS = ["W_top1", "W_top2", "L0_rec_w0", "L0_rec_w1", "L0_rec_w2"]
_COLUMNS = ["L0_rec_b0", "L0_rec_b1", "L0_rec_b2", "b_top1", "b_top2", "W_top3"]


def kernel(**inputs):
    import numpy as np
    import concourse.bacc as bacc
    from concourse.bass_utils import run_bass_kernel_spmd

    nc = bacc.Bacc("TRN2", target_bir_lowering=False, num_devices=1)
    arrays, ins = {}, {}
    columns = np.concatenate([np.asarray(inputs[name]).reshape(-1, P).T for name in _COLUMNS], axis=1)
    for name in ["dense_ctx", "ids", "columns"] + _TABLES + _WEIGHTS:
        a = np.ascontiguousarray(columns if name == "columns" else inputs[name])
        if name == "ids":
            a = np.concatenate([a, a[:P]], axis=0)
        arrays[f"in_{name}"] = a
        ins[name] = nc.dram_tensor(f"in_{name}", a.shape, mybir.dt.from_np(a.dtype), kind="ExternalInput").ap()
    y = nc.dram_tensor("y", (BATCH, 1), F32, kind="ExternalOutput").ap()
    build(nc, ins, y)
    r = run_bass_kernel_spmd(nc, [arrays], core_ids=[0])
    return r.results[0]["y"]
```

```python
from contextlib import ExitStack

import concourse.bass as bass
from concourse import mybir

F32 = mybir.dt.float32
F32R = mybir.dt.float32r
I32 = mybir.dt.int32
ALU = mybir.AluOpType
ACT = mybir.ActivationFunctionType

P = 128
FIELDS = 39
D = 16
BATCH = 2048
HALF = 64
BLOCKS = BATCH // P
CHUNK = 512
DPC = CHUNK // P
STEPS = D // DPC
BCOLS = D * P
PITCH = BATCH * D + 1024
TILES = 20
SHIFTS = 3
TILES0 = 7
ROWS0 = SHIFTS * FIELDS
LAST0 = 2 * FIELDS

VECTOR = {1: "FDPlFDPFlPDFl", 0: "PFPF", 2: "DPFlPDPlDPlDFl"}
TENSOR = {
    1: "h0 h1 l1 h3 h2 l2 h4 h5 h6 l4 l5 h7 h9 h8 l8 l7",
    0: "h1 h0 l0 h3 h2 l2",
    2: "h2 h0 h1 l1 l0 h4 l4 h3 l3 h5 h6 l6 h7 h8 l8 l5 h9 l7",
}
GROUPS = [2, 4, 6, 9]
SCALAR_AT = {
    "unstage": (1, 1), "top3": (1, 2), "maps2": (1, 4), "rep": (1, 6), "maps1": (0, 1), "top1": (0, 2),
    "dense": (2, 2), "top2": (2, 4), "group0": (2, 4), "group1": (2, 5), "group2": (2, 6), "maps0": (2, 7),
    "group3": (2, 7),
}
POOL_AT = {
    "finish2": (1, 3), "add2": (0, 0), "add01": (2, 0),
}
RF, RPZ, RPH, RPL, RDH, RDL = 2, 3, 3, 2, 2, 2
DOUBLE = 5
SLOTS = [
    2, 1, 0, 1, 2, 1, 1, 1, 1,
    1, 3, 0, 2, 0, 2, 2, 0, 0,
    2, 2, 0, 1, 1, 1, 1, 1, 1,
    2, 1, 1, 1, 0, 1, 1, 1, 1,
]
LATE_SLOTS, EARLY_FROM = 23, 25
STAGED, EARLY = sum(SLOTS[LATE_SLOTS:EARLY_FROM]), sum(SLOTS[EARLY_FROM:])

LAYERS = (1, 0, 2)
PAIRS = {layer: [(kind, VECTOR[layer].replace("l", "")[:p].count(kind))
                 for p, kind in enumerate(VECTOR[layer].replace("l", ""))] for layer in LAYERS}
ORDER = {layer: [(x[0], int(x[1:])) for x in TENSOR[layer].split()] for layer in LAYERS}
BEFORE = {kind: {layer: sum(VECTOR[x].count(kind) for x in LAYERS[:LAYERS.index(layer)]) for layer in LAYERS}
          for kind in "FDP"}
PER_STEP = {kind: sum(VECTOR[x].count(kind) for x in LAYERS) for kind in "FDP"}
AHEAD = {kind: VECTOR[0].count(kind) for kind in "FDP"}


def tiles_of(layer, pos):
    return 1 if layer == 0 and pos == 3 else 2


def build(nc, ins, y_out):
    x0_dram = nc.dram_tensor("x0_scratch", [2 * FIELDS, PITCH], F32).ap()
    w0c_dram = nc.dram_tensor("w0_columns_twice", [FIELDS, 2 * FIELDS, P], F32).ap()
    w0r_dram = nc.dram_tensor("w0_rows_twice", [2 * FIELDS, FIELDS, P], F32).ap()

    with ExitStack() as ctx:
        def sb(name, shape, dt=F32):
            return ctx.enter_context(nc.sbuf_tensor(name, shape, dt))

        def ps(name, shape):
            return ctx.enter_context(nc.psum_tensor(name, shape, F32))

        def sem(name):
            return ctx.enter_context(nc.semaphore(name))

        bcA = sb("bcA", [P, 2, 2 * DOUBLE, CHUNK])
        bcB = sb("bcB", [P, TILES - 2 * DOUBLE, CHUNK])
        rot = sb("rot", [ROWS0, TILES0, CHUNK])
        rep = sb("rep", [ROWS0, CHUNK])
        zF = sb("zF", [P, RF, 2, CHUNK])
        zP = sb("zP", [P, RPZ, 2, CHUNK])
        hiP = sb("hiP", [P, RPH, 2, CHUNK], F32R)
        loP = sb("loP", [P, RPL, 2, CHUNK], F32R)
        hiD = sb("hiD", [P, RDH, 2, CHUNK], F32R)
        loD = sb("loD", [P, RDL, 2, CHUNK], F32R)
        n_f = sum(tiles_of(layer, p) for layer in LAYERS for p, (kind, _) in enumerate(PAIRS[layer]) if kind == "F")
        n_r = TILES0 + 2 * TILES - n_f
        wF = sb("wF", [P, n_f, P])
        wH = sb("wH", [P, n_r, P], F32R)
        wL = sb("wL", [P, n_r, P], F32R)
        columns = sb("columns", [P, 11])
        bias, bt1, bt2, wt3 = columns[:, 0:3], columns[:, 3:7], columns[:, 7:9], columns[:, 9:11]
        ids_sb = sb("ids_sb", [P, FIELDS], I32)
        emb = sb("emb", [P, FIELDS, D])
        ids_next = sb("ids_next", [P, STAGED], I32)
        emb_next = sb("emb_next", [P, STAGED, D])
        dense = sb("dense", [P, D])
        ident = sb("ident", [P, P])
        small = sb("small", [HALF + 1, 2, CHUNK])
        x0T = small[:FIELDS, :, :]
        y_sb = small[HALF:HALF + 1, 0, 0:P]
        denseT = sb("denseT", [D, P])
        sum01 = sb("sum01", [P, CHUNK])
        sum2 = sb("sum2", [P, CHUNK])
        dir01 = sb("dir01", [P, CHUNK])
        dir2 = sb("dir2", [P, CHUNK])
        zsum = sb("zsum", [P, 2, P])
        wt1 = sb("wt1", [P, 2, 512])
        wt1d = sb("wt1d", [D, 512])
        wt2 = sb("wt2", [P, 4, 256])
        h1 = sb("h1", [P, 4, P])
        h2 = sb("h2", [P, 2, P])

        acc = ps("acc", [P, 2, CHUNK])
        xk1 = ps("xk1", [P, CHUNK])
        xk2 = ps("xk2", [P, CHUNK])
        repP = ps("repP", [P, CHUNK])
        zD = ps("zD", [P, 2, CHUNK])
        misc = ps("misc", [P, CHUNK])

        stage = bcA[:, :, :, :].rearrange("p a t n -> p (a t n)")
        raw1 = stage[:, 0:TILES * P].rearrange("p (t s) -> p t s", s=P)
        raw2 = stage[:, TILES * P:2 * TILES * P].rearrange("p (t s) -> p t s", s=P)
        o = 2 * TILES * P
        symA = stage[:ROWS0, o:o + TILES0 * P].rearrange("p (t s) -> p t s", s=P)
        symB = stage[:ROWS0, o + TILES0 * P:o + 2 * TILES0 * P].rearrange("p (t s) -> p t s", s=P)

        s_w0c = sem("s_w0_columns_twice")
        s_w0r = sem("s_w0_rows_twice")
        s_sym = sem("s_sym_in")
        s_raw = sem("s_raw_in")
        s_small = sem("s_small_in")
        s_edge = sem("s_edge_zeroed")
        s_added = sem("s_sym_added")
        s_wh = sem("s_weights_hi")
        s_wl = sem("s_weights_split")
        s_id0 = sem("s_ident_zeroed")
        s_id = sem("s_ident_ready")
        s_ids = sem("s_ids_in")
        s_gather = sem("s_gathered")
        s_ids_next = sem("s_ids_next_in")
        s_staged = sem("s_staged_gathered")
        s_unstaged = sem("s_staged_moved")
        s_tr = sem("s_transposed")
        s_trout = sem("s_transposes_read")
        s_x0w = [sem(f"s_x0_written{g}") for g in range(STEPS)]
        s_dense = sem("s_dense_in")
        s_rot = sem("s_rot_in")
        s_rep = sem("s_rep_in_psum")
        s_bcA = [sem(f"s_bcA_in{p}") for p in range(2)]
        s_bcB = [sem(f"s_bcB_in{p}") for p in range(2)]
        s_mulF = sem("s_mulF")
        s_mulP = sem("s_mulP")
        s_mulD = sem("s_mulD")
        s_hiP = sem("s_hiP")
        s_hiD = sem("s_hiD")
        s_loP = sem("s_loP")
        s_loD = sem("s_loD")
        s_usedF = sem("s_usedF")
        s_usedP = sem("s_usedP")
        s_usedD = sem("s_usedD")
        s_out = sem("s_acc_read")
        s_xk1 = sem("s_xk1_ready")
        s_xk2 = sem("s_xk2_ready")
        s_add01 = sem("s_dir01_added")
        s_add2 = sem("s_dir2_added")
        s_half01 = sem("s_sum01_halved")
        s_half2 = sem("s_sum2_halved")
        s_z01 = sem("s_zsum01_ready")
        s_z2 = sem("s_zsum2_ready")
        s_top = sem("s_top_psum")
        s_topr = sem("s_top_read")
        s_y = sem("s_y_out")

        class Step:

            def __init__(self, b, k, tail=False):
                self.b, self.k, self.tail = b, k, tail

            def n(self, kind, layer, i):
                cut = AHEAD[kind] if self.tail and layer == 2 else 0
                return AHEAD[kind] + PER_STEP[kind] * self.k + BEFORE[kind][layer] + i - cut

            def count(self, kind, local):
                return PER_STEP[kind] * STEPS * self.b + local

            def stage(self, layer):
                return 1 + 3 * self.k + {1: 0, 0: 1, 2: 2}[layer] - (1 if self.tail and layer == 2 else 0)

            def steps(self):
                return self.b * STEPS + self.k

        class Ahead(Step):

            def __init__(self):
                super().__init__(0, 0)

            def n(self, kind, layer, i):
                return i

            def stage(self, layer):
                return 0

            def steps(self):
                return -1

        def wait_count(eng, s, value):
            if isinstance(value, int) and value <= 0:
                return
            eng.wait_ge(s, value)

        def multiplied(st, layer, pos):
            kind, i = pairs_of(layer)[pos]
            return {"F": s_mulF, "D": s_mulD, "P": s_mulP}[kind], st.count(kind, st.n(kind, layer, i) + 1)

        def gathered(b):
            return 16 * (FIELDS - STAGED) * (b - 1) + 2 * 16 * FIELDS

        def in_registers(eng, *values):
            return [v if isinstance(v, int) else eng.to_reg(v) for v in values]

        def pairs_of(layer):
            return PAIRS[layer]

        def rows_of(layer, pos):
            return P if layer else (LAST0 if pos == 3 else ROWS0)

        def bc_pair(st, pos):
            if pos < DOUBLE:
                return bcA[:, st.k % 2, 2 * pos:2 * pos + 2, :]
            q = pos - DOUBLE
            return bcB[:, 2 * q:2 * q + 2, :]

        def weight(layer, pos, j):
            kind, _ = PAIRS[layer][pos]
            before = [(x, p) for x in LAYERS for p in range(len(PAIRS[x]))]
            before = before[:before.index((layer, pos))]
            return kind, sum(tiles_of(x, p) for x, p in before if (PAIRS[x][p][0] == "F") == (kind == "F")) + j

        def weights_of(layer):
            rows = P if layer else ROWS0
            raw = (symA, raw1, raw2)[layer]
            for pos in range(len(pairs_of(layer))):
                kind, w = weight(layer, pos, 0)
                tiles = tiles_of(layer, pos)
                yield kind, raw[:, 2 * pos:2 * pos + tiles, :], slice(w, w + tiles), rows

        def run(engine, body):
            body(0)
            with engine.Fori(1, BLOCKS - 1) as b:
                body(b)
            body(BLOCKS - 1)

        def first(b):
            return isinstance(b, int) and b == 0

        def last(b):
            return isinstance(b, int) and b == BLOCKS - 1

        def is_tail(b, k):
            return last(b) and k == STEPS - 1

        block = ctx.enter_context(nc.Block())

        @block.sync
        def _(sp):
            def load_ids(b):
                sp.dma_start(ids_sb[:, :], ins["ids"][bass.ds(b * P, P), :]).then_inc(s_ids, 16)

            def load_ids_next(b):
                sp.dma_start(ids_next[:, :], ins["ids"][bass.ds(b * P, P), 0:STAGED]).then_inc(s_ids_next, 16)

            def load_dense(b):
                sp.dma_start(dense[:, :], ins["dense_ctx"][bass.ds(b * P, P), :]).then_inc(s_dense, 16)

            def x0_rows(row, col, dims):
                return bass.AP(tensor=x0_dram.tensor, offset=col + row * PITCH, ap=dims)

            def load_rot(b, k):
                col = b * BCOLS + k * CHUNK
                for j in range(SHIFTS):
                    sp.dma_start(rot[j * FIELDS:(j + 1) * FIELDS, :, :],
                                 x0_rows(j, col, [[PITCH, FIELDS], [SHIFTS * PITCH, TILES0], [1, CHUNK]])
                                 ).then_inc(s_rot, 16)
                for j in range(SHIFTS):
                    sp.dma_start(rep[j * FIELDS:(j + 1) * FIELDS, :],
                                 x0_rows(0, col, [[PITCH, FIELDS], [1, CHUNK]])).then_inc(s_rot, 16)

            def load_bcA(b, k):
                col = b * BCOLS + k * CHUNK
                for h in range(2):
                    sp.dma_start(bcA[h * HALF:(h + 1) * HALF, k % 2, :, :],
                                 x0_rows(h, col, [[0, HALF], [2 * PITCH, 2 * DOUBLE], [1, CHUNK]])
                                 ).then_inc(s_bcA[k % 2], 16)

            def load_bcB(b, k, part):
                lo, hi = [(DOUBLE, 7), (7, 10)][part]
                col = b * BCOLS + k * CHUNK
                for h in range(2):
                    sp.dma_start(bcB[h * HALF:(h + 1) * HALF, 2 * (lo - DOUBLE):2 * (hi - DOUBLE), :],
                                 x0_rows(4 * lo + h, col, [[0, HALF], [2 * PITCH, 2 * (hi - lo)], [1, CHUNK]])
                                 ).then_inc(s_bcB[part], 16)

            def write_x0(b, g):
                col = b * BCOLS + g * CHUNK
                for twice in range(2):
                    sp.dma_start(x0_dram[twice * FIELDS:(twice + 1) * FIELDS, bass.ds(col, CHUNK)],
                                 x0T[:, g % 2, :]).then_inc(s_x0w[g], 16)

            load_ids(0)
            w0 = ins["L0_rec_w0"]
            for twice in range(2):
                sp.dma_start(w0c_dram[:, twice * FIELDS:(twice + 1) * FIELDS, :], w0).then_inc(s_w0c, 16)
                sp.dma_start(w0r_dram[twice * FIELDS:(twice + 1) * FIELDS, :, :], w0).then_inc(s_w0r, 16)
            for layer, raw in ((1, raw1), (2, raw2)):
                w = ins[f"L0_rec_w{layer}"].rearrange("h k s -> (h k) s")
                sp.dma_start(raw[:, 0:TILES - 1, :],
                             w[0:(TILES - 1) * P, :].rearrange("(t p) s -> p t s", p=P)).then_inc(s_raw, 16)
                sp.dma_start(raw[0:HALF, TILES - 1, :], w[(TILES - 1) * P:FIELDS * HALF, :]).then_inc(s_raw, 16)
            sp.wait_ge(s_w0c, 32)
            sp.wait_ge(s_w0r, 32)
            for j in range(SHIFTS):
                sp.dma_start(symA[j * FIELDS:(j + 1) * FIELDS, :, :],
                             bass.AP(tensor=w0c_dram.tensor, offset=j * P,
                                     ap=[[(2 * FIELDS + 1) * P, FIELDS], [SHIFTS * P, TILES0], [1, P]])
                             ).then_inc(s_sym, 16)
                sp.dma_start(symB[j * FIELDS:(j + 1) * FIELDS, :, :],
                             bass.AP(tensor=w0r_dram.tensor, offset=j * FIELDS * P,
                                     ap=[[(FIELDS + 1) * P, FIELDS], [SHIFTS * FIELDS * P, TILES0], [1, P]])
                             ).then_inc(s_sym, 16)
            sp.dma_start(columns[:, :], ins["columns"]).then_inc(s_small, 16)
            sp.dma_start(wt1[:, :, :], ins["W_top1"][0:2 * P, :].rearrange("(t p) n -> p t n", p=P)).then_inc(s_small, 16)
            sp.dma_start(wt1d[:, :], ins["W_top1"][2 * P:2 * P + D, :]).then_inc(s_small, 16)
            sp.dma_start(wt2[:, :, :], ins["W_top2"].rearrange("(t p) n -> p t n", p=P)).then_inc(s_small, 16)

            for g in range(STEPS):
                sp.wait_ge(s_trout, g + 1)
                write_x0(0, g)
                if g == 1:
                    sp.wait_ge(s_x0w[0], 32)
                    load_rot(0, 0)
                    sp.wait_ge(s_wl, 3)
                    load_bcA(0, 0)
            sp.wait_ge(s_gather, 16 * FIELDS)
            load_ids(1)
            load_bcB(0, 0, 0)
            load_bcB(0, 0, 1)
            sp.wait_ge(*multiplied(Ahead(), 0, 3))
            sp.wait_ge(s_x0w[1], 32)
            load_rot(0, 1)

            def body(b):
                for k in range(STEPS):
                    st = Step(b, k, is_tail(b, k))
                    nb, nk = (b, k + 1) if k < STEPS - 1 else (b + 1, 0)
                    rb, rk = (b, k + 2) if k < STEPS - 2 else (b + 1, k - 2)
                    if not is_tail(b, k):
                        s, v = multiplied(st, 2, DOUBLE - 1)
                        used, written = in_registers(sp, v - PER_STEP[PAIRS[2][DOUBLE - 1][0]], 32 * nb + 32)
                        wait_count(sp, s, used)
                        sp.wait_ge(s_x0w[nk], written)
                        load_bcA(nb, nk)
                    if k == 0:
                        wait_count(sp, s_tr, 5 * b + 4)
                        load_dense(b)
                    if k == 1 and not last(b):
                        wait_count(sp, s_staged, 16 * STAGED * b)
                        load_ids_next(b + 2)
                    if k == 3 and not first(b):
                        sp.wait_ge(s_topr, 3 * b)
                        sp.dma_start(y_out[bass.ds(b * P - P, P), :].rearrange("n a -> a n"), y_sb[:, :]).then_inc(s_y, 16)
                    if k == 2 and not last(b):
                        sp.wait_ge(s_gather, gathered(b + 1))
                        load_ids(b + 2)
                        for g in range(STEPS - 1):
                            sp.wait_ge(s_trout, 5 * b + 6 + g)
                            write_x0(b + 1, g)
                    if k == 2 and not last(b):
                        sp.wait_ge(*multiplied(st, 2, 6))
                        load_bcB(nb, nk, 0)
                        sp.wait_ge(s_trout, 5 * b + 9)
                        write_x0(b + 1, STEPS - 1)
                    if not (last(b) and k >= STEPS - 2):
                        s, v = multiplied(st, 0, 3)
                        used, written = in_registers(sp, v, 32 * rb + 32)
                        sp.wait_ge(s, used)
                        sp.wait_ge(s_x0w[rk], written)
                        load_rot(rb, rk)
                    if not is_tail(b, k):
                        if k != 2 or last(b):
                            sp.wait_ge(*multiplied(st, 2, 6))
                            load_bcB(nb, nk, 0)
                        sp.wait_ge(*multiplied(st, 2, 9))
                        load_bcB(nb, nk, 1)

            run(sp, body)
            sp.wait_ge(s_topr, 3 * BLOCKS)
            sp.dma_start(y_out[BATCH - P:BATCH, :].rearrange("n a -> a n"), y_sb[:, :]).then_inc(s_y, 16)
            sp.wait_ge(s_y, 16 * BLOCKS)

        @block.gpsimd
        def _(pool):
            nc.gpsimd.memset(ident[:, :], 0.0).then_inc(s_id0, 1)
            pool.wait_ge(s_id0, 1)
            nc.gpsimd.affine_select(out=ident[:, :], in_=ident[:, :], compare_op=ALU.not_equal, fill=1.0, base=0,
                                    pattern=[[-1, P]], channel_multiplier=1).then_inc(s_id, 1)

            def gather(field, ids, rows, landed):
                pool.indirect_dma_start(rows[:, field, :], None, ins[f"tbl_{field}"][:, :],
                                        bass.IndirectOffsetOnAxis(ap=ids[:, field:field + 1], axis=0)
                                        ).then_inc(landed, 16)

            def low(st, layer, i):
                n = st.n("P", layer, i)
                rows = P if layer else ROWS0
                pool.wait_ge(s_hiP, st.count("P", n + 1))
                wait_count(pool, s_usedP, st.count("P", n + 1 - RPL))
                nc.gpsimd.tensor_tensor(loP[:rows, n % RPL, :, :], zP[:rows, n % RPZ, :, :],
                                        hiP[:rows, n % RPH, :, :].bitcast(F32), ALU.subtract).then_inc(s_loP, 1)

            def finish2(b):
                pool.wait_ge(s_out, 12 * b + 13 - (1 if last(b) else 0))
                pool.wait_ge(s_add2, 3 * b + 2)
                nc.gpsimd.tensor_tensor(sum2[:, :], sum2[:, :], dir2[:, :], ALU.add).then_inc(s_add2, 1)
                pool.wait_ge(s_add2, 3 * b + 3)
                nc.gpsimd.tensor_tensor(sum2[:, 0:2 * P], sum2[:, 0:2 * P], sum2[:, 2 * P:4 * P],
                                        ALU.add).then_inc(s_half2, 1)
                pool.wait_ge(s_half2, b + 1)
                nc.gpsimd.tensor_tensor(zsum[:, 1, :], sum2[:, 0:P], sum2[:, P:2 * P], ALU.add).then_inc(s_z2, 1)

            pool.wait_ge(s_ids, 16)
            for f in range(FIELDS):
                gather(f, ids_sb, emb, s_gather)
            for i in range(AHEAD["P"]):
                low(Ahead(), 0, i)

            def body(b):
                fields = [] if last(b) else list(range(0 if first(b) else STAGED + EARLY, FIELDS)) + \
                    list(range(STAGED + EARLY))
                late_slots, late = sum(n > 0 for n in SLOTS[:LATE_SLOTS]), len(fields) - STAGED - EARLY
                slots, seen = list(SLOTS), 0
                if first(b):
                    for q in range(LATE_SLOTS):
                        if SLOTS[q]:
                            slots[q] = (seen + 1) * late // late_slots - seen * late // late_slots
                            seen += 1

                def gathers(slot):
                    for n in range(sum(slots[:slot]), sum(slots[:slot + 1])):
                        if n >= len(fields):
                            continue
                        if late <= n < late + STAGED:
                            gather(fields[n], ids_next, emb_next, s_staged)
                        else:
                            gather(fields[n], ids_sb, emb, s_gather)

                def before_gathers(slot):
                    if first(b) and slot == 0:
                        pool.wait_ge(s_ids, 32)
                        pool.wait_ge(s_tr, 4)
                    if slot == LATE_SLOTS and not last(b):
                        pool.wait_ge(s_ids_next, 16 * b + 16)
                        wait_count(pool, s_unstaged, b)
                    if slot == EARLY_FROM and not last(b):
                        pool.wait_ge(s_ids, 16 * b + 48)
                        pool.wait_ge(s_tr, 5 * b + 9)

                def task(name, k):
                    if name == "finish2" and k == 0 and not first(b):
                        finish2(b - 1)
                    if name == "add2" and k >= 2:
                        pool.wait_ge(s_out, 12 * b + Step(b, k).stage(1))
                        pool.wait_ge(s_add2, 3 * b + k - 2) if k == 3 else wait_count(pool, s_add2, 3 * b)
                        nc.gpsimd.tensor_tensor(sum2[:, :], sum2[:, :], dir2[:, :], ALU.add).then_inc(s_add2, 1)
                    if name == "add01" and k > 0:
                        pool.wait_ge(s_out, 12 * b + Step(b, k).stage(1) + 1)
                        wait_count(pool, s_add01, 3 * b + k - 1)
                        nc.gpsimd.tensor_tensor(sum01[:, :], sum01[:, :], dir01[:, :], ALU.add).then_inc(s_add01, 1)
                    if name == "add01" and k == STEPS - 1:
                        pool.wait_ge(s_add01, 3 * b + 3)
                        nc.gpsimd.tensor_tensor(sum01[:, 0:2 * P], sum01[:, 0:2 * P], sum01[:, 2 * P:4 * P],
                                                ALU.add).then_inc(s_half01, 1)
                        pool.wait_ge(s_half01, b + 1)
                        nc.gpsimd.tensor_tensor(zsum[:, 0, :], sum01[:, 0:P], sum01[:, P:2 * P],
                                                ALU.add).then_inc(s_z01, 1)

                for k in range(STEPS):
                    st, slot = Step(b, k, is_tail(b, k)), k * PER_STEP["P"]
                    for layer in LAYERS:
                        lows = VECTOR[layer].count("P")
                        for i in range(lows + 1):
                            for name, at in POOL_AT.items():
                                if at == (layer, i):
                                    task(name, k)
                            if i < lows and not (layer == 0 and is_tail(b, k)):
                                before_gathers(slot)
                                low(st, layer, i)
                                gathers(slot)
                            if i < lows:
                                slot += 1

            run(pool, body)
            finish2(BLOCKS - 1)

        @block.scalar
        def _(act):
            act.wait_ge(s_added, 1)
            def split_weights(layer):
                for kind, raw, w, rows in weights_of(layer):
                    dst = (wF if kind == "F" else wH)[:rows, w, :]
                    a = nc.scalar.activation(dst, raw, ACT.Copy)
                a.then_inc(s_wh, 1)

            split_weights(0)
            act.wait_ge(s_raw, 64)
            act.wait_ge(s_edge, 1)
            split_weights(1)
            split_weights(2)

            def high(st, layer, kind, i):
                n = st.n(kind, layer, i)
                rows = P if layer else ROWS0
                if kind == "P":
                    act.wait_ge(s_mulP, st.count("P", n + 1))
                    wait_count(act, s_usedP, st.count("P", n + 1 - RPH))
                    nc.scalar.activation(hiP[:rows, n % RPH, :, :], zP[:rows, n % RPZ, :, :],
                                         ACT.Copy).then_inc(s_hiP, 1)
                else:
                    act.wait_ge(s_mulD, st.count("D", n + 1))
                    wait_count(act, s_usedD, st.count("D", n + 1 - RDH))
                    nc.scalar.activation(hiD[:rows, n % RDH, :, :], zD[:rows, :, :], ACT.Copy).then_inc(s_hiD, 1)

            def maps(st, layer, b, k):
                n = st.stage(layer)
                kind, i = PAIRS[layer][ORDER[layer][-1][1]]
                act.wait_ge({"F": s_usedF, "D": s_usedD, "P": s_usedP}[kind], st.count(kind, st.n(kind, layer, i) + 1))
                src = acc[:, n % 2, :]
                if layer < 2:
                    xk, ready = ((xk1, s_xk1), (xk2, s_xk2))[layer]
                    for h in range(2):
                        nc.scalar.activation(xk[h * HALF:(h + 1) * HALF, :], src[0:HALF, :], ACT.Relu,
                                             bias=bias[0:HALF, layer:layer + 1]).then_inc(ready, 1)
                    wait_count(act, s_z01, b) if k == 0 else wait_count(act, s_add01, 3 * b + k - 1)
                    dst = sum01 if k == 0 else dir01
                    nc.scalar.activation(dst[layer * HALF:(layer + 1) * HALF, :], src[HALF:P, :], ACT.Relu,
                                         bias=bias[HALF:P, layer:layer + 1]).then_inc(s_out, 1)
                else:
                    wait_count(act, s_z2, b) if k == 0 else wait_count(act, s_add2, 3 * b + k - 1)
                    dst = sum2 if k == 0 else dir2
                    nc.scalar.activation(dst[:, :], src, ACT.Relu, bias=bias[:, 2:3]).then_inc(s_out, 1)

            def rep_to_psum(c):
                act.wait_ge(s_rot, 96 * c + 96)
                nc.scalar.activation(repP[:ROWS0, :], rep[:, :], ACT.Copy).then_inc(s_rep, 1)

            def transposed(b, g, n):
                act.wait_ge(s_tr, n)
                wait_count(act, s_x0w[(g - 2) % STEPS], 32 * b + (32 if g >= 2 else 0))
                nc.scalar.activation(x0T[:, g % 2, :], misc[:FIELDS, :], ACT.Copy).then_inc(s_trout, 1)

            transposed(0, 0, 1)
            transposed(0, 1, 2)
            rep_to_psum(0)
            transposed(0, 2, 3)
            transposed(0, 3, 4)
            act.wait_ge(s_small, 64)
            for kind, i in PAIRS[0]:
                if kind != "F":
                    high(Ahead(), 0, kind, i)
            maps(Ahead(), 0, 0, 0)

            def relu_top(dst, n, b_col):
                for m in range(n):
                    a = nc.scalar.activation(dst[:, m, :], misc[:, m * P:(m + 1) * P], ACT.Relu,
                                             bias=b_col[:, m:m + 1])
                return a

            def body(b):
                def task(name, k):
                    st = Step(b, k, is_tail(b, k))
                    if name == "maps2" and not (first(b) and k == 0):
                        before = Step(b, k - 1) if k else Step(b - 1, STEPS - 1)
                        maps(before, 2, before.b, before.k)
                    if name == "top3" and k == 2 and not first(b):
                        act.wait_ge(s_top, 3 * b)
                        wait_count(act, s_y, 16 * b - 16)
                        nc.scalar.activation(y_sb, misc[0:1, 0:P], ACT.Copy).then_inc(s_topr, 1)
                    if name == "unstage" and k == 3 and not last(b):
                        act.wait_ge(s_staged, 16 * STAGED * b + 16 * STAGED)
                        act.wait_ge(s_tr, 5 * b + 9)
                        nc.scalar.activation(emb[:, 0:STAGED, :], emb_next[:, :, :], ACT.Copy).then_inc(s_unstaged, 1)
                    if name == "rep" and not is_tail(b, k):
                        rep_to_psum(st.steps() + 1)
                    if name == "maps1":
                        maps(st, 1, b, k)
                    if name == "top1" and k == 0 and not first(b):
                        act.wait_ge(s_top, 3 * b - 2)
                        relu_top(h1, 4, bt1).then_inc(s_topr, 1)
                    if name == "dense" and k == 2:
                        act.wait_ge(s_tr, 5 * b + 5)
                        wait_count(act, s_top, 3 * b - 2)
                        nc.scalar.activation(denseT[:, :], misc[:D, 0:P], ACT.Copy).then_inc(s_trout, 1)
                    if name == "maps0" and not is_tail(b, k):
                        nb, nk = (b, k + 1) if k < STEPS - 1 else (b + 1, 0)
                        maps(st, 0, nb, nk)
                    if name == "top2" and k == 1 and not first(b):
                        act.wait_ge(s_top, 3 * b - 1)
                        relu_top(h2, 2, bt2).then_inc(s_topr, 1)
                    if name.startswith("group") and k == 2 and not last(b):
                        g = int(name[5:])
                        transposed(b + 1, g, 5 * b + 6 + g)

                for k in range(STEPS):
                    st = Step(b, k, is_tail(b, k))
                    for layer in LAYERS:
                        highs = [x for x in PAIRS[layer] if x[0] != "F"]
                        for n in range(len(highs) + 1):
                            for name, at in SCALAR_AT.items():
                                if at == (layer, n):
                                    task(name, k)
                            if n < len(highs) and not (layer == 0 and is_tail(b, k)):
                                high(st, layer, *highs[n])

            run(act, body)
            maps(Step(BLOCKS - 1, STEPS - 1, True), 2, BLOCKS - 1, STEPS - 1)
            act.wait_ge(s_top, 3 * BLOCKS - 2)
            relu_top(h1, 4, bt1).then_inc(s_topr, 1)
            act.wait_ge(s_top, 3 * BLOCKS - 1)
            relu_top(h2, 2, bt2).then_inc(s_topr, 1)
            act.wait_ge(s_top, 3 * BLOCKS)
            act.wait_ge(s_y, 16 * BLOCKS - 16)
            nc.scalar.activation(y_sb, misc[0:1, 0:P], ACT.Copy).then_inc(s_topr, 1)

        @block.vector
        def _(dve):
            nc.vector.memset(raw1[HALF:P, TILES - 1, :], 0.0)
            nc.vector.memset(raw2[HALF:P, TILES - 1, :], 0.0).then_inc(s_edge, 1)
            dve.wait_ge(s_sym, 96)
            nc.vector.memset(symB[0:FIELDS, 0, :], 0.0).then_inc(s_edge, 1)
            dve.wait_ge(s_edge, 2)
            nc.vector.tensor_tensor(symA[:, :, :], symA[:, :, :], symB[:, :, :], ALU.add).then_inc(s_added, 1)
            for layer in range(3):
                dve.wait_ge(s_wh, layer + 1)
                for kind, raw, w, rows in weights_of(layer):
                    if kind != "F":
                        a = nc.vector.tensor_tensor(wL[:rows, w, :], raw, wH[:rows, w, :].bitcast(F32), ALU.subtract)
                a.then_inc(s_wl, 1)

            def multiply(st, layer, pos):
                kind, i = pairs_of(layer)[pos]
                n, rows, tiles = st.n(kind, layer, i), rows_of(layer, pos), tiles_of(layer, pos)
                if layer == 0:
                    x0, xk = rot[:rows, 2 * pos:2 * pos + tiles, :], repP
                else:
                    x0, xk = bc_pair(st, pos), (xk1, xk2)[layer - 1]
                xk = xk[:rows, :].unsqueeze(1).broadcast_to([rows, tiles, CHUNK])
                if kind == "F":
                    wait_count(dve, s_usedF, st.count("F", n + 1 - RF))
                    nc.vector.tensor_tensor(zF[:rows, n % RF, 0:tiles, :], x0, xk, ALU.mult).then_inc(s_mulF, 1)
                elif kind == "P":
                    wait_count(dve, s_loP, st.count("P", n + 1 - RPZ))
                    nc.vector.tensor_tensor(zP[:rows, n % RPZ, 0:tiles, :], x0, xk, ALU.mult).then_inc(s_mulP, 1)
                else:
                    wait_count(dve, s_loD, st.count("D", n))
                    nc.vector.tensor_tensor(zD[:rows, 0:tiles, :], x0, xk, ALU.mult).then_inc(s_mulD, 1)

            def low(st, layer, i):
                n = st.n("D", layer, i)
                dve.wait_ge(s_hiD, st.count("D", n + 1))
                wait_count(dve, s_usedD, st.count("D", n + 1 - RDL))
                rows = P if layer else ROWS0
                nc.vector.tensor_tensor(loD[:rows, n % RDL, :, :], zD[:rows, :, :],
                                        hiD[:rows, n % RDH, :, :].bitcast(F32),
                                        ALU.subtract).then_inc(s_loD, 1)

            def run_layer(st, layer, c=None):
                if layer == 0:
                    dve.wait_ge(s_rot, 96 * c + 96)
                    dve.wait_ge(s_rep, c + 1)
                else:
                    dve.wait_ge((s_xk1, s_xk2)[layer - 1], 2 * st.steps() + 2)
                pos = lows = 0
                for op in VECTOR[layer]:
                    if op == "l":
                        low(st, layer, lows)
                        lows += 1
                        continue
                    if layer == 1 and pos == 0:
                        dve.wait_ge(s_bcA[st.k % 2], 32 * (2 * st.b + st.k // 2 + 1))
                    if layer == 1 and pos in (DOUBLE, 7):
                        dve.wait_ge(s_bcB[pos >= 7], 32 * st.steps() + 32)
                    multiply(st, layer, pos)
                    pos += 1

            run_layer(Ahead(), 0, 0)

            def body(b):
                for k in range(STEPS):
                    st = Step(b, k, is_tail(b, k))
                    for layer in LAYERS:
                        if not (layer == 0 and is_tail(b, k)):
                            run_layer(st, layer, st.steps() + 1)

            run(dve, body)

        @block.tensor
        def _(pe):
            pe.wait_ge(s_id, 1)

            def accumulate(st, layer, q):
                order = ORDER[layer]
                part, pos = order[q]
                kind, i = pairs_of(layer)[pos]
                n, rows, stage_n = st.n(kind, layer, i), rows_of(layer, pos), st.stage(layer)
                begin, end = q == 0, q == len(order) - 1
                if begin:
                    wait_count(pe, s_out, 12 * st.b + stage_n - 1)
                if kind == "F":
                    z, ready, used, weights = zF[:rows, n % RF], s_mulF, s_usedF, [wF]
                elif kind == "P":
                    z = hiP[:rows, n % RPH] if part == "h" else loP[:rows, n % RPL]
                    ready, used = (s_hiP if part == "h" else s_loP), s_usedP
                else:
                    z = hiD[:rows, n % RDH] if part == "h" else loD[:rows, n % RDL]
                    ready, used = (s_hiD if part == "h" else s_loD), s_usedD
                if kind != "F":
                    weights = [wL, wH] if part == "h" else [wH]
                pe.wait_ge(ready, st.count(kind, n + 1))
                terms = [(x[:rows, weight(layer, pos, j)[1], :], z[:, j, :])
                         for j in range(tiles_of(layer, pos)) for x in weights]
                for t, (w, x) in enumerate(terms):
                    mm = nc.tensor.matmul(acc[:, stage_n % 2, :], w, x, start=begin and t == 0,
                                          stop=end and t == len(terms) - 1)
                if kind == "F" or part == "l":
                    mm.then_inc(used, 1)

            def run_layer0(st):
                for q in range(len(ORDER[0])):
                    accumulate(st, 0, q)

            def transposes(g):
                for j in range(DPC):
                    t = nc.tensor.transpose(misc[:FIELDS, j * P:(j + 1) * P], emb[:, :, DPC * g + j], ident[:, :])
                t.then_inc(s_tr, 1)

            for g in range(STEPS):
                pe.wait_ge(s_gather, 16 * FIELDS)
                wait_count(pe, s_trout, g)
                transposes(g)
            pe.wait_ge(s_wl, 3)
            run_layer0(Ahead())

            def top1(b):
                pe.wait_ge(s_trout, 5 * b + (9 if not last(b) else 5))
                pe.wait_ge(s_z01, b + 1)
                pe.wait_ge(s_z2, b + 1)
                pe.wait_ge(s_small, 64)
                wait_count(pe, s_topr, 3 * b)
                for m in range(4):
                    cols = slice(m * P, (m + 1) * P)
                    for t in range(2):
                        nc.tensor.matmul(misc[:, cols], wt1[:, t, cols], zsum[:, t, :], start=(t == 0), stop=False)
                    mm = nc.tensor.matmul(misc[:, cols], wt1d[:, cols], denseT[:, :], start=False, stop=True)
                mm.then_inc(s_top, 1)

            def top2(b):
                pe.wait_ge(s_topr, 3 * b + 1)
                for m in range(2):
                    for t in range(4):
                        mm = nc.tensor.matmul(misc[:, m * P:(m + 1) * P], wt2[:, t, m * P:(m + 1) * P], h1[:, t, :],
                                              start=(t == 0), stop=(t == 3))
                mm.then_inc(s_top, 1)

            def top3(b):
                pe.wait_ge(s_topr, 3 * b + 2)
                for t in range(2):
                    mm = nc.tensor.matmul(misc[0:1, 0:P], wt3[:, t:t + 1], h2[:, t, :], start=(t == 0), stop=(t == 1))
                mm.then_inc(s_top, 1)

            def body(b):
                for k in range(STEPS):
                    st = Step(b, k, is_tail(b, k))
                    for q in range(len(ORDER[1])):
                        accumulate(st, 1, q)
                    if k == 0 and not first(b):
                        top1(b - 1)
                    if not is_tail(b, k):
                        run_layer0(st)
                    if k == 1 and not first(b):
                        top2(b - 1)
                    if k == 2:
                        pe.wait_ge(s_dense, 16 * b + 16)
                        wait_count(pe, s_trout, 5 * b + 4)
                        wait_count(pe, s_topr, 3 * b)
                        nc.tensor.transpose(misc[:D, 0:P], dense[:, :], ident[:, :]).then_inc(s_tr, 1)
                    for q in range(len(ORDER[2])):
                        group = k == 2 and not last(b) and q in GROUPS
                        if group:
                            g = GROUPS.index(q)
                            if g == 0:
                                pe.wait_ge(s_gather, gathered(b + 1))
                                wait_count(pe, s_unstaged, b)
                            pe.wait_ge(s_trout, 5 * b + 5 + g)
                        accumulate(st, 2, q)
                        if group:
                            transposes(g)
                    if k == 1 and not first(b):
                        top3(b - 1)

            run(pe, body)
            top1(BLOCKS - 1)
            top2(BLOCKS - 1)
            top3(BLOCKS - 1)


_TABLES = [f"tbl_{i}" for i in range(FIELDS)]
_WEIGHTS = ["W_top1", "W_top2", "L0_rec_w0", "L0_rec_w1", "L0_rec_w2"]
_COLUMNS = ["L0_rec_b0", "L0_rec_b1", "L0_rec_b2", "b_top1", "b_top2", "W_top3"]


def kernel(**inputs):
    import numpy as np
    import concourse.bacc as bacc
    from concourse.bass_utils import run_bass_kernel_spmd

    nc = bacc.Bacc("TRN2", target_bir_lowering=False, num_devices=1)
    arrays, ins = {}, {}
    columns = np.concatenate([np.asarray(inputs[name]).reshape(-1, P).T for name in _COLUMNS], axis=1)
    for name in ["dense_ctx", "ids", "columns"] + _TABLES + _WEIGHTS:
        a = np.ascontiguousarray(columns if name == "columns" else inputs[name])
        if name == "ids":
            a = np.concatenate([a, a[:P]], axis=0)
        arrays[f"in_{name}"] = a
        ins[name] = nc.dram_tensor(f"in_{name}", a.shape, mybir.dt.from_np(a.dtype), kind="ExternalInput").ap()
    y = nc.dram_tensor("y", (BATCH, 1), F32, kind="ExternalOutput").ap()
    build(nc, ins, y)
    r = run_bass_kernel_spmd(nc, [arrays], core_ids=[0])
    return r.results[0]["y"]
```
